# Optimizing a Trainium2 kernel written in Bass

```python
import numpy as np
import jax
import jax.numpy as jnp

def _softmax(x, axis=-1):
    return jax.nn.softmax(x, axis=axis)

def _gelu(x):
    return jax.nn.gelu(x, approximate=True)

def _silu(x):
    return jax.nn.silu(x)

def _sigmoid(x):
    return jax.nn.sigmoid(x)

def _layernorm(x, axis=-1, eps=1e-05):
    m = jnp.mean(x, axis=axis, keepdims=True)
    v = jnp.var(x, axis=axis, keepdims=True)
    return (x - m) / jnp.sqrt(v + eps)

def _scatter_add(tgt, idx, src, axis=0):
    return tgt.at[idx].add(src)

def _segment_sum(src, seg, n):
    return jax.ops.segment_sum(src, seg, n)
kernel_name = 'mk_gnn_resnorm_d1_gnn_r32_cd2db8'

def setup_inputs(seed: int=0):
    np.random.seed(seed)
    _w = jnp.asarray

    def _rec_inputs():
        import jax
        import jax.numpy as jnp
        _gk = jax.random.key(seed)
        x = -6.415e-05 + 1 * jax.random.normal(jax.random.fold_in(_gk, 1), (10000, 512), jnp.float32)
        src = jax.random.randint(jax.random.fold_in(_gk, 2), (5000,), 0, 10000, jnp.int32)
        dst = jnp.minimum((10000 * jax.random.uniform(jax.random.fold_in(_gk, 3), (5000,)) ** 2.0).astype(jnp.int32), 9999)
        _o = jnp.argsort(dst, stable=True)
        src = src[_o]
        dst = dst[_o]
        return (x, src, dst)
    x, src, dst = _rec_inputs()

    def _L0_gnn_setup():
        import jax, jax.numpy as jnp
        import numpy as np
        N, E, DM, H, DFF = (625, 20000, 512, 8, 64)
        DK = DM // H

        def _layernorm(x, g, b, eps=1e-05):
            mu = jnp.mean(x, axis=-1, keepdims=True)
            var = jnp.mean(jnp.square(x - mu), axis=-1, keepdims=True)
            return (x - mu) * jax.lax.rsqrt(var + eps) * g + b
        key = jax.random.key(seed)
        ks = jax.random.split(key, 12)
        s = 0.02
        h = jax.random.normal(ks[0], (N, DM), dtype=jnp.float32)
        src = jax.random.randint(ks[1], (E,), 0, N, dtype=jnp.int32)
        dst = jnp.sort(jax.random.randint(ks[2], (E,), 0, N, dtype=jnp.int32))
        return {'h': h, 'src': src, 'dst': dst, 'Wq': jax.random.normal(ks[3], (DM, DM), dtype=jnp.float32) * s, 'Wk': jax.random.normal(ks[4], (DM, DM), dtype=jnp.float32) * s, 'Wv': jax.random.normal(ks[5], (DM, DM), dtype=jnp.float32) * s, 'Wo': jax.random.normal(ks[6], (DM, DM), dtype=jnp.float32) * s, 'ln1_g': jnp.ones((DM,), jnp.float32), 'ln1_b': jnp.zeros((DM,), jnp.float32), 'ln2_g': jnp.ones((DM,), jnp.float32), 'ln2_b': jnp.zeros((DM,), jnp.float32), 'W1': jax.random.normal(ks[7], (DM, DFF), dtype=jnp.float32) * s, 'b1': jnp.zeros((DFF,), jnp.float32), 'W2': jax.random.normal(ks[8], (DFF, DM), dtype=jnp.float32) * s, 'b2': jnp.zeros((DM,), jnp.float32)}
    _L0_gnn_all = _L0_gnn_setup()
    _L0_gnn_in = {k: v for k, v in _L0_gnn_all.items() if k in ('Wq', 'Wk', 'Wv', 'Wo', 'ln1_g', 'ln1_b', 'ln2_g', 'ln2_b', 'W1', 'b1', 'W2', 'b2')}
    del _L0_gnn_all
    return {'x': x, 'src': src, 'dst': dst, 'L0_gnn_Wq': _L0_gnn_in['Wq'], 'L0_gnn_Wk': _L0_gnn_in['Wk'], 'L0_gnn_Wv': _L0_gnn_in['Wv'], 'L0_gnn_Wo': _L0_gnn_in['Wo'], 'L0_gnn_ln1_g': _L0_gnn_in['ln1_g'], 'L0_gnn_ln1_b': _L0_gnn_in['ln1_b'], 'L0_gnn_ln2_g': _L0_gnn_in['ln2_g'], 'L0_gnn_ln2_b': _L0_gnn_in['ln2_b'], 'L0_gnn_W1': _L0_gnn_in['W1'], 'L0_gnn_b1': _L0_gnn_in['b1'], 'L0_gnn_W2': _L0_gnn_in['W2'], 'L0_gnn_b2': _L0_gnn_in['b2']}

def reference(x, src, dst, L0_gnn_Wq, L0_gnn_Wk, L0_gnn_Wv, L0_gnn_Wo, L0_gnn_ln1_g, L0_gnn_ln1_b, L0_gnn_ln2_g, L0_gnn_ln2_b, L0_gnn_W1, L0_gnn_b1, L0_gnn_W2, L0_gnn_b2):
    import jax
    import jax.numpy as jnp

    def _L0_gnn_ref(h, src, dst, Wq, Wk, Wv, Wo, ln1_g, ln1_b, ln2_g, ln2_b, W1, b1, W2, b2):
        import jax, jax.numpy as jnp
        import numpy as np
        N, E, DM, H, DFF = (625, 20000, 512, 8, 64)
        DK = DM // H

        def _layernorm(x, g, b, eps=1e-05):
            mu = jnp.mean(x, axis=-1, keepdims=True)
            var = jnp.mean(jnp.square(x - mu), axis=-1, keepdims=True)
            return (x - mu) * jax.lax.rsqrt(var + eps) * g + b
        n = h.shape[0]
        q = (h @ Wq).reshape(n, H, DK)
        k = (h @ Wk).reshape(n, H, DK)
        v = (h @ Wv).reshape(n, H, DK)
        e = jnp.einsum('ehd,ehd->eh', k[src], q[dst]) / np.sqrt(DK).astype(np.float32)
        m = jax.ops.segment_max(e, dst, num_segments=n)
        ex = jnp.exp(e - m[dst])
        z = jax.ops.segment_sum(ex, dst, num_segments=n)
        attn = ex / z[dst]
        a = jax.ops.segment_sum(attn[:, :, None] * v[src], dst, num_segments=n)
        a = a.reshape(n, DM)
        o = a @ Wo
        x = _layernorm(h + o, ln1_g, ln1_b)
        f = jax.nn.relu(x @ W1 + b1) @ W2 + b2
        return _layernorm(x + f, ln2_g, ln2_b)
    x = _layernorm(x + _L0_gnn_ref(x, src, dst, L0_gnn_Wq, L0_gnn_Wk, L0_gnn_Wv, L0_gnn_Wo, L0_gnn_ln1_g, L0_gnn_ln1_b, L0_gnn_ln2_g, L0_gnn_ln2_b, L0_gnn_W1, L0_gnn_b1, L0_gnn_W2, L0_gnn_b2), axis=-1)
    return x

_drawn_inputs = setup_inputs


def setup_inputs(seed=0):
    import zlib

    import numpy as np

    out = dict(_drawn_inputs(seed))
    spreads = {'L0_gnn_ln1_g': (1.0, 0.2),
     'L0_gnn_ln1_b': (0.0, 0.1),
     'L0_gnn_ln2_g': (1.0, 0.2),
     'L0_gnn_ln2_b': (0.0, 0.1),
     'L0_gnn_b1': (0.0, 0.8),
     'L0_gnn_b2': (0.0, 0.1)}
    factors = {'L0_gnn_Wq': 8.0, 'L0_gnn_Wk': 8.0}
    for name, (base, spread) in spreads.items():
        noise = np.random.default_rng([zlib.crc32(name.encode()), seed]).standard_normal(out[name].shape)
        drawn = base * np.exp(spread * noise) if base else spread * noise
        out[name] = jnp.asarray(drawn.astype(out[name].dtype))
    for name, factor in factors.items():
        out[name] = (out[name] * factor).astype(out[name].dtype)
    return out
```

```python
from contextlib import ExitStack

import concourse.bass as bass
from concourse import mybir

F32 = mybir.dt.float32
F32R = mybir.dt.float32r
BF16 = mybir.dt.bfloat16
I32 = mybir.dt.int32
U32 = mybir.dt.uint32
ALU = mybir.AluOpType
ACT = mybir.ActivationFunctionType

HEADS = 8
EPS = 1e-5
SKIP = 1 << 20
FAR = 3.0e38

ROUND = [
    "A.sum1", "TXD", "A.norm1", "B.sum1", "Q0", "A.T", "Q1", "A.F1", "Q2", "B.norm1", "Q3", "TXS",
    "A.F2", "B.T", "A.norm2", "K0", "B.F1", "K1", "A.sum3", "K2", "A.norm3", "K3", "B.F2", "C.sum1",
    "S", "B.norm2", "C.norm1", "V0", "C.T", "ZT", "B.sum3", "V1", "RZ", "C.F1", "B.norm3", "D.sum1",
    "V2", "D.norm1", "C.F2", "V3", "C.norm2", "D.T", "C.sum3", "D.F1", "C.norm3", "O0", "O1",
    "E0.sum1", "D.F2", "O2", "E0.norm1", "D.norm2", "O3", "E0.T", "D.sum3", "E0.F1", "E1.sum1",
    "D.norm3", "E1.norm1", "E0.F2", "E1.T", "E0.norm2", "E1.F1", "E0.sum3", "E1.F2", "E0.norm3",
    "E1.norm2", "E1.sum3", "E1.norm3",
]
SLOTS = ["A", "B", "C", "D", "E0", "E1"]
JOBS = len(SLOTS)
FILLS = 4 + 4 + 2 * JOBS


def graph_attention(nc, x, src, dst, Wq, Wk, Wv, Wo, g1, be1, g2, be2, W1, b1, W2, b2, out):
    N, D = x.shape
    E = src.shape[0]
    DFF = W1.shape[1]
    P = 128
    KC = D // P
    HD = P // HEADS
    DK = D // HEADS
    ET = 125
    EG = KC * ET
    ROUNDS = E // EG
    NB = 2 * P
    TAIL = (N - (4 * ROUNDS - 1) * NB) // 2
    CT = E // ET
    CN = 8 * ROUNDS
    assert E == ROUNDS * EG and N <= 4 * ROUNDS * NB and TAIL > 0 and D == 512 and 2 * DFF == P

    ctx = ExitStack()
    with ctx:
        def sb(name, shape, dt=F32):
            return ctx.enter_context(nc.sbuf_tensor(name, shape, dt))

        def sem(name):
            return ctx.enter_context(nc.semaphore(name))

        ident = sb("ident", [P, P])
        same_head = sb("same_head", [P, P])
        wq = [sb(f"wq_{n}", [P, KC, D], F32R) for n in ("hi", "lo")]
        wk = [sb(f"wk_{n}", [P, KC, D], F32R) for n in ("hi", "lo")]
        wv = [sb(f"wv_{n}", [P, KC, D], F32R) for n in ("hi", "lo")]
        wo = [sb(f"wo_{n}", [P, KC, D], F32R) for n in ("hi", "lo")]
        w1 = [sb(f"w1_{n}", [P, KC, P], F32R) for n in ("hi", "lo")]
        w2 = [sb(f"w2_{n}", [P, D], F32R) for n in ("hi", "lo")]
        bias2 = sb("bias2", [P, D], F32R)
        ones = sb("ones", [P, P], F32R)
        g1_all = sb("g1_all", [P, D])
        g2_all = sb("g2_all", [P, D])
        be2_all = sb("be2_all", [P, D])
        g1_col = sb("g1_col", [P, KC])
        be1_col = sb("be1_col", [P, KC])
        b1_col = sb("b1_col", [P, 1])
        eps_col = sb("eps_col", [P, 1])
        src_idx = sb("src_idx", [ET, CT], I32)
        dst_idx = sb("dst_idx", [ET, CT], I32)
        last_idx = sb("last_idx", [ET, CT], I32)
        node_idx = sb("node_idx", [P, CN], I32)
        src_now = sb("src_now", [ET, 4], I32)
        dst_now = sb("dst_now", [ET, 4], I32)
        erow_now = sb("erow_now", [ET, 4], I32)
        last_now = sb("last_now", [ET, 4], I32)
        node_now = sb("node_now", [P, 8], I32)
        xs = sb("xs", [ET, 4, D])
        xd = sb("xd", [ET, 4, D])
        xT = [sb(f"xT_{n}", [P, KC, EG], F32R) for n in ("hi", "lo")]
        q = sb("q", [P, KC, D])
        qk = sb("qk", [P, EG])
        qk_m = sb("qk_m", [P, EG])
        dst_row = sb("dst_row", [P, EG + 1], I32)
        far = sb("far", [P, EG])
        nsame = sb("nsame", [P, EG])
        mx = sb("mx", [P, EG + 1])
        zs = sb("zs", [P, EG + 1])
        ex = sb("ex", [P, 2, EG])
        rz = sb("rz", [ET, 4, HEADS])
        rz_all = q[0:ET, 0, :].rearrange("p (t n) -> p t n", t=4)
        wgt = sb("wgt", [P, 2, EG])
        att = sb("att", [P, 2, EG])
        carry = sb("carry", [P, KC])
        aT = [sb(f"aT_{n}", [P, KC, EG], F32R) for n in ("hi", "lo")]
        xin = [sb(f"xin{n}", [P, 2, D]) for n in range(2)]
        xb = [sb(f"xb{n}", [P, 2, D]) for n in range(2)]
        rows = sb("rows", [P, 8, D])
        n1, x2, y, z = (rows[:, 2 * n:2 * n + 2, :] for n in range(4))
        nT = [sb(f"nT_{n}", [P, KC, NB], F32R) for n in ("hi", "lo")]
        h_relu = sb("h_relu", [P, NB])
        hT = sb("hT", [P, NB], F32R)
        st = [sb(f"st{n}", [P, 2, 6]) for n in (1, 2, 3)]
        mv = [sb(f"mv{n}", [P, 2, 2]) for n in (1, 2, 3)]
        sd = [sb(f"sd{n}", [P, 2]) for n in (1, 2, 3)]
        rs = [sb(f"rs{n}", [P, 2]) for n in (1, 2, 3)]
        nm = [sb(f"nm{n}", [P, 2]) for n in (1, 2, 3)]

        pT = [ctx.enter_context(nc.psum_tensor(f"pT{n}", [P, 512], F32)) for n in range(2)]
        pP = [ctx.enter_context(nc.psum_tensor(f"pP{n}", [P, 512], F32)) for n in range(2)]
        pS = ctx.enter_context(nc.psum_tensor("pS", [P, 512], F32))
        pZ = ctx.enter_context(nc.psum_tensor("pZ", [P, 512], F32))
        pF = [ctx.enter_context(nc.psum_tensor(f"pF{n}", [P, 512], F32)) for n in range(2)]

        w_stage = {"q": q[:, :, :], "k": rows[:, 0:4, :], "o": rows[:, 4:8, :], "v": q[:, :, :]}
        w1_raw = xin[0][:, 0, 0:KC * DFF].rearrange("p (k f) -> p k f", k=KC)
        w1_scaled = xin[0][:, 1, 0:KC * DFF].rearrange("p (k f) -> p k f", k=KC)
        w2_raw = xin[1][:, 0, :]
        b_raw = xb[0]
        b_sum = xb[1][:, 0, :]
        idx_raw = ex[:, :, :].rearrange("p a b -> p (a b)")[:, 0:3 * ET].bitcast(I32).rearrange("p (a b) -> p a b", a=3)
        idx_f = ex[:, :, :].rearrange("p a b -> p (a b)")[:, 512:512 + 3 * ET].rearrange("p (a b) -> p a b", a=3)
        OHT = 10
        oh_p = att[:, :, :].rearrange("p a b -> p (a b)").bitcast(BF16)[0:ET, 0:OHT * P].rearrange("p (t n) -> p t n", t=OHT)
        oh_c = wgt[:, :, :].rearrange("p a b -> p (a b)").bitcast(BF16)[0:ET, 0:OHT * CN].rearrange("p (t n) -> p t n", t=OHT)
        iota_n = qk[:, 0:P]
        iota_i = qk_m[:, 0:P].bitcast(I32)
        node_i = qk_m[:, P:P + CN].bitcast(I32)
        part_i = qk[:, P:P + CT].bitcast(I32)
        col_i = qk[:, 2 * P:2 * P + CT].bitcast(I32)
        low_i = qk[:, 3 * P:3 * P + CT].bitcast(I32)
        part_f = qk_m[:, 2 * P:2 * P + CT]
        col_f = qk_m[:, 2 * P + CT:2 * P + 2 * CT]
        has_edge = qk_m[:, 3 * P:3 * P + CN]

        names = """idx_loaded wq_loaded wk_loaded wv_loaded wo_loaded w1_loaded w2_loaded b_loaded all_loaded
        row_loaded ident_set ident_done head_set head_done zero_set idx_cast idx_turned idx_done last_flag
        split_hi split_lo w1_scale w1_hi w1_lo w2_hi w2_lo b1_folded b1_done bias_sum bias_hi bias_lo ones_set
        iota_set iota_cast digit_low digit_col digit_done onehot counted flag_done node_done init_done
        gate_sp gate_pool gate_act gate_dve
        src_picked dst_picked erow_picked last_picked node_picked xs_loaded xd_loaded xin_loaded0 xin_loaded1
        erow_loaded0 erow_loaded1 mask_eq mask_done
        tr_filled tr_hi tr_lo pj_filled q_saved qk_part qk_acc qk_done score_done max_done max_carried
        decay_half decay_done weight_exp exp_done z_done z_carried zT_done rz_done rz_spread rzb_done beta_done alpha_done
        weighted scanned carried a_hi a_lo
        hx_done st1_done mv1_done sd1_done rs1_done nm1_done n1_done xb_done xr_done
        h_filled relu_done h_hi h_lo f_filled x2_done
        st2_done mv2_done sd2_done rs2_done nm2_done n2_done y_done s_done
        st3_done mv3_done sd3_done rs3_done nm3_done z_rows out_node out_edge""".split()
        s = {name: sem(name) for name in names}

        block = ctx.enter_context(nc.Block())

        def bcast_rows(ap, n):
            return bass.AP(tensor=ap.tensor, offset=ap.offset, ap=[[0, P], [1, n]])

        @block.sync
        def _(sp):
            def gate(name, value):
                sp.wait_ge(s[name], value)
                sp.sem_inc(s["gate_sp"], 1)

            def rows_of(block_no, parts=P):
                return x[bass.ds(NB * block_no, 2 * parts), :].rearrange("(p t) d -> p t d", t=2)

            def load_dst_row(i):
                sp.dma_start(dst_row[:, :], bass.AP(tensor=dst.tensor, offset=dst.offset + (EG * i - 1), ap=[[0, P], [1, EG + 1]]))\
                    .then_inc(s["row_loaded"], 16)

            sp.dma_start(idx_raw[0:CT, 0, :], src.rearrange("(t e) -> t e", e=ET)).then_inc(s["idx_loaded"], 16)
            sp.dma_start(idx_raw[0:CT, 1, :], dst.rearrange("(t e) -> t e", e=ET)).then_inc(s["idx_loaded"], 16)
            sp.wait_ge(s["zero_set"], 2)
            sp.dma_start(idx_raw[0:CT - 1, 2, :], dst[1:1 + (CT - 1) * ET].rearrange("(t e) -> t e", e=ET))\
                .then_inc(s["idx_loaded"], 16)
            sp.dma_start(idx_raw[CT - 1:CT, 2, 0:ET - 1], dst[1 + (CT - 1) * ET:E].rearrange("(t e) -> t e", t=1))\
                .then_inc(s["idx_loaded"], 16)
            sp.dma_start(w_stage["q"], Wq.rearrange("(k p) n -> p k n", p=P)).then_inc(s["wq_loaded"], 16)
            with nc.allow_non_contiguous_dma("short columns, once"):
                sp.dma_start(g1_col[:, :], g1.rearrange("(k p) -> p k", p=P)).then_inc(s["w1_loaded"], 16)
                sp.dma_start(be1_col[:, :], be1.rearrange("(k p) -> p k", p=P)).then_inc(s["w1_loaded"], 16)
                for half in range(2):
                    sp.dma_start(b1_col[DFF * half:DFF * half + DFF, :], b1.rearrange("(f a) -> f a", a=1))\
                        .then_inc(s["w1_loaded"], 16)
            sp.dma_start(w1_raw, W1.rearrange("(k p) f -> p k f", p=P)).then_inc(s["w1_loaded"], 16)
            for half in range(2):
                sp.dma_start(w2_raw[DFF * half:DFF * half + DFF, :], W2).then_inc(s["w2_loaded"], 16)
            sp.dma_start(dst_row[:, 1:EG + 1], bcast_rows(dst, EG)).then_inc(s["row_loaded"], 16)
            sp.dma_start(w_stage["k"], Wk.rearrange("(k p) n -> p k n", p=P)).then_inc(s["wk_loaded"], 16)
            sp.wait_ge(s["zero_set"], 3)
            for row in (0, 32):
                sp.dma_start(b_raw[row:row + 1, 0, :], b2.rearrange("(a n) -> a n", a=1)).then_inc(s["b_loaded"], 16)
                sp.dma_start(b_raw[row:row + 1, 1, :], be1.rearrange("(a n) -> a n", a=1)).then_inc(s["b_loaded"], 16)
            for tile, vec in ((g1_all, g1), (be2_all, be2), (g2_all, g2)):
                sp.dma_start(tile[:, :], bcast_rows(vec, D)).then_inc(s["all_loaded"], 16)
            wo_rows = Wo.rearrange("(h m d) n -> h d m n", h=HEADS, m=KC)
            for h in range(HEADS):
                sp.dma_start(w_stage["o"][HD * h:HD * h + HD, :, :], wo_rows[h]).then_inc(s["wo_loaded"], 16)
            sp.wait_ge(s["split_lo"], KC)
            sp.dma_start(w_stage["v"], Wv.rearrange("(k p) n -> p k n", p=P)).then_inc(s["wv_loaded"], 16)
            sp.wait_ge(s["b1_folded"], 1)
            sp.wait_ge(s["w1_lo"], 2)
            sp.wait_ge(s["w2_lo"], 1)
            for n in range(2):
                sp.dma_start(xin[n][:, :, :], rows_of(n)).then_inc(s[f"xin_loaded{n}"], 16)

            def round_loads(i, last):
                for n in range(2):
                    gate("n1_done", JOBS * i + n + 1)
                    gate("xb_done", JOBS * i + n + 1)
                    gate("mv1_done", 2 * (JOBS * i + n + 1))
                    parts = TAIL if last and n == 1 else P
                    sp.dma_start(xin[n][0:parts, :, :], rows_of(4 * i + 2 + n, parts)).then_inc(s[f"xin_loaded{n}"], 16)
                if last:
                    return
                gate("mask_eq", i + 1)
                load_dst_row(i + 1)
                for n in range(2):
                    gate("hx_done", 4 * i + 2 * n + 2)
                    gate("xb_done", JOBS * i + 4 + n + 1)
                    sp.dma_start(xin[n][:, :, :], rows_of(4 * i + 4 + n)).then_inc(s[f"xin_loaded{n}"], 16)

            with sp.Fori(0, ROUNDS - 1) as i:
                round_loads(i, last=False)
            round_loads(ROUNDS - 1, last=True)

        @block.gpsimd
        def _(pool):
            def gate(name, value):
                pool.wait_ge(s[name], value)
                pool.sem_inc(s["gate_pool"], 1)

            pool.memset(idx_raw[0:64, 2, :], -1).then_inc(s["zero_set"], 1)
            pool.memset(dst_row[:, 0:1], -1).then_inc(s["zero_set"], 1)
            pool.memset(b_raw[:, :, :], 0.0).then_inc(s["zero_set"], 1)
            pool.memset(ident[:, :], 0.0).then_inc(s["ident_set"], 1)
            pool.memset(same_head[:, :], DK ** -0.5).then_inc(s["head_set"], 1)
            pool.wait_ge(s["ident_set"], 1)
            pool.affine_select(out=ident[:, :], in_=ident[:, :], compare_op=ALU.not_equal, fill=1.0, base=0,
                               pattern=[[-1, P]], channel_multiplier=1).then_inc(s["ident_done"], 1)
            heads = same_head[:, :].rearrange("p (h d) -> p h d", h=HEADS)
            pool.wait_ge(s["head_set"], 1)
            pool.affine_select(out=heads, in_=heads, compare_op=ALU.is_ge, fill=0.0, base=0,
                               pattern=[[-HD, HEADS], [0, HD]], channel_multiplier=1).then_inc(s["head_set"], 1)
            pool.wait_ge(s["head_set"], 2)
            pool.affine_select(out=heads, in_=heads, compare_op=ALU.is_ge, fill=0.0, base=HD - 1,
                               pattern=[[HD, HEADS], [0, HD]], channel_multiplier=-1).then_inc(s["head_done"], 1)
            pool.iota(iota_i, pattern=[[1, P]], base=0, channel_multiplier=0).then_inc(s["iota_set"], 1)
            pool.iota(node_i.rearrange("p (b t) -> p b t", t=2), pattern=[[NB, CN // 2], [1, 2]], base=0,
                      channel_multiplier=2).then_inc(s["iota_set"], 1)
            pool.memset(eps_col[:, :], EPS).then_inc(s["init_done"], 1)
            pool.memset(mx[:, 0:1], 0.0).then_inc(s["init_done"], 1)
            pool.memset(zs[:, 0:1], 0.0).then_inc(s["init_done"], 1)
            pool.memset(carry[:, :], 0.0).then_inc(s["init_done"], 1)

            def pick(now, table, name, i, width, free=None):
                if free:
                    gate(*free)
                pool.tensor_copy(now[:, :], table[:, bass.ds(width * i, width)]).then_inc(s[name], 1)

            def gather(dest, index, name):
                pool.indirect_dma_start(dest, None, x, bass.IndirectOffsetOnAxis(ap=index.bitcast(U32), axis=0),
                                        bounds_check=N - 1, oob_is_err=False).then_inc(s[name], 16)

            def scatter(rows_ap, index, name):
                pool.indirect_dma_start(out, bass.IndirectOffsetOnAxis(ap=index.bitcast(U32), axis=0), rows_ap, None,
                                        bounds_check=N - 1, oob_is_err=False).then_inc(s[name], 16)

            def gather_group(i, first):
                pick(dst_now, dst_idx, "dst_picked", i, 4, None if first else ("xd_loaded", 64 * i))
                gate("dst_picked", i + 1)
                if not first:
                    gate("tr_filled", FILLS * (i - 1) + TXD_END)
                for t in range(4):
                    gather(xd[:, t, :], dst_now[:, t:t + 1], "xd_loaded")
                pick(src_now, src_idx, "src_picked", i, 4, None if first else ("xs_loaded", 64 * i))
                gate("src_picked", i + 1)
                if not first:
                    gate("tr_filled", FILLS * (i - 1) + TXS_END)
                for t in range(4):
                    gather(xs[:, t, :], src_now[:, t:t + 1], "xs_loaded")

            fills, TXD_END, TXS_END = 0, 0, 0
            for step in ROUND:
                fills += 4 if step in ("TXD", "TXS") else 2 if step.endswith(".T") else 0
                TXD_END = fills if step == "TXD" else TXD_END
                TXS_END = fills if step == "TXS" else TXS_END

            pool.wait_ge(s["idx_done"], 3)
            gather_group(0, first=True)

            def one_round(i, last):
                def masks():
                    gate("mask_eq", i + 1)
                    gate("decay_done", i)
                    pool.tensor_scalar(far[:, :], nsame[:, :], FAR, -FAR, ALU.mult, ALU.add).then_inc(s["mask_done"], 1)
                    gate("mask_done", 2 * i + 1)
                    pool.tensor_scalar(nsame[:, :], nsame[:, :], -1.0, 0.0, ALU.mult, ALU.add).then_inc(s["mask_done"], 1)

                for step in ROUND:
                    if step == "TXD":
                        masks()
                        pick(erow_now, dst_idx, "erow_picked", i, 4, ("erow_loaded1", 32 * i))
                        pick(last_now, last_idx, "last_picked", i, 4, ("out_edge", 64 * i))
                        if isinstance(i, int) and i == 0:
                            pool.wait_ge(s["node_done"], 1)
                        pick(node_now, node_idx, "node_picked", i, 8, ("out_node", 128 * i))
                    elif step[0] == "K" and step != "K0":
                        m = int(step[1])
                        gate("qk_part", 4 * i + m + 1)
                        if m > 1:
                            gate("qk_acc", 3 * i + m - 1)
                        pool.tensor_tensor(qk[:, :], qk[:, :], qk_m[:, :], ALU.add).then_inc(s["qk_acc"], 1)
                    elif step == "S":
                        gate("mask_done", 2 * i + 2)
                        gate("max_done", i + 1)
                        gate("scanned", 4 * i)
                        pool.tensor_tensor(ex[:, 0, :], mx[:, 0:EG], far[:, :], ALU.add).then_inc(s["decay_half"], 1)
                        gate("decay_half", i + 1)
                        pool.tensor_tensor(ex[:, 0, :], ex[:, 0, :], mx[:, 1:EG + 1], ALU.subtract).then_inc(s["decay_done"], 1)
                        gate("decay_done", i + 1)
                        gate("weight_exp", i + 1)
                        pool.tensor_copy(mx[:, 0:1], mx[:, EG:EG + 1]).then_inc(s["max_carried"], 1)
                    elif step == "V3" and not last:
                        gather_group(i + 1, first=False)
                    if "." not in step:
                        continue
                    slot, what = step.split(".")
                    n = SLOTS.index(slot)
                    j = JOBS * i + n
                    edge = slot[0] == "E"
                    R = ET if edge else P
                    if what == "norm1":
                        if edge:
                            gate(f"erow_loaded{n % 2}", 32 * (i + 1))
                        else:
                            gate(f"xin_loaded{n % 2}", 16 * (2 * i + n // 2 + 1))
                        gate("s_done", j)
                        pool.tensor_tensor(xb[n % 2][0:R, :, :], xin[n % 2][0:R, :, :],
                                           be2_all[0:R, :].rearrange("p (a d) -> p a d", a=1).broadcast_to([R, 2, D]), ALU.add)\
                            .then_inc(s["xb_done"], 1)
                        if slot == "C" or slot == "D":
                            e = n - 2
                            if slot == "C":
                                gate("erow_picked", i + 1)
                            gate("xb_done", j + 1)
                            gate("n1_done", j + 1)
                            for t in range(2):
                                gather(xin[e][0:ET, t, :], erow_now[:, 2 * e + t:2 * e + t + 1], f"erow_loaded{e}")
                    elif what == "F1":
                        gate("n1_done", j + 1)
                        gate("n2_done", j)
                        pool.tensor_tensor(x2[0:R, :, :], n1[0:R, :, :],
                                           g1_all[0:R, :].rearrange("p (a d) -> p a d", a=1).broadcast_to([R, 2, D]), ALU.mult)\
                            .then_inc(s["xr_done"], 1)
                    elif what == "norm2":
                        gate("n2_done", j + 1)
                        pool.tensor_tensor(y[0:R, :, :], y[0:R, :, :],
                                           g2_all[0:R, :].rearrange("p (a d) -> p a d", a=1).broadcast_to([R, 2, D]), ALU.mult)\
                            .then_inc(s["y_done"], 1)
                        gate("y_done", j + 1)
                        pool.tensor_tensor(y[0:R, :, :], y[0:R, :, :], xb[n % 2][0:R, :, :], ALU.add).then_inc(s["s_done"], 1)
                    elif what == "norm3":
                        gate("z_rows", j + 1)
                        gate("last_picked" if edge else "node_picked", i + 1)
                        for t in range(2):
                            if edge:
                                scatter(z[0:R, t, :], last_now[:, 2 * (n - 4) + t:2 * (n - 4) + t + 1], "out_edge")
                            else:
                                scatter(z[0:R, t, :], node_now[:, 2 * n + t:2 * n + t + 1], "out_node")

            pool.wait_ge(s["all_loaded"], 48)
            pool.sem_inc(s["s_done"], 1)
            pool.wait_ge(s["node_done"], 1)
            with pool.Fori(0, ROUNDS - 1) as i:
                one_round(i, last=False)
            one_round(ROUNDS - 1, last=True)
            pool.wait_ge(s["out_node"], 128 * ROUNDS)
            pool.wait_ge(s["out_edge"], 64 * ROUNDS)

        @block.scalar
        def _(act):
            def gate(name, value):
                act.wait_ge(s[name], value)
                act.sem_inc(s["gate_act"], 1)

            def by_head(ap, k):
                return ap[:, k, :].rearrange("p (h m d) -> p m h d", h=HEADS, m=KC)

            def split_hi(w, stage, loaded, permute):
                act.wait_ge(s[loaded], 16 if loaded != "wo_loaded" else 16 * HEADS)
                for k in range(KC):
                    dest = w[0][:, k, :]
                    if permute:
                        act.activation(dest.rearrange("p (m h d) -> p m h d", m=KC, h=HEADS), by_head(stage, k), ACT.Copy)\
                            .then_inc(s["split_hi"], 1)
                    else:
                        act.activation(dest, stage[:, k, :], ACT.Copy).then_inc(s["split_hi"], 1)

            split_hi(wq, w_stage["q"], "wq_loaded", True)
            act.wait_ge(s["w1_scale"], KC)
            for half in range(2):
                act.activation(w1[0][:, :, DFF * half:DFF * half + DFF], w1_scaled, ACT.Copy).then_inc(s["w1_hi"], 1)
            act.wait_ge(s["w2_loaded"], 32)
            act.activation(w2[0][:, :], w2_raw, ACT.Copy).then_inc(s["w2_hi"], 1)
            split_hi(wk, w_stage["k"], "wk_loaded", True)
            act.wait_ge(s["bias_sum"], 1)
            act.activation(bias2[:, :], b_sum, ACT.Copy).then_inc(s["bias_hi"], 1)
            split_hi(wv, w_stage["v"], "wv_loaded", True)
            split_hi(wo, w_stage["o"], "wo_loaded", False)
            act.wait_ge(s["init_done"], 4)

            def one_round(i):
                fill = 0
                used = 0
                for step in ROUND:
                    if step in ("TXD", "TXS"):
                        for k in range(KC):
                            gate("tr_filled", FILLS * i + fill + 1)
                            if step == "TXD":
                                gate("pj_filled", 16 * i)
                            else:
                                gate("pj_filled", 16 * i + 4)
                            act.activation(xT[0][:, k, :], pT[fill % 2][:, 0:EG], ACT.Copy).then_inc(s["tr_hi"], 1)
                            fill += 1
                    elif step[0] == "Q":
                        m = int(step[1])
                        gate("pj_filled", 16 * i + used + 1)
                        gate("rzb_done", i)
                        act.activation(q[:, m, 0:EG], pP[used % 2][:, 0:EG], ACT.Copy).then_inc(s["q_saved"], 1)
                    elif step == "S":
                        gate("decay_done", i + 1)
                        gate("weight_exp", i + 1)
                        act.activation(ex[:, :, :], ex[:, :, :], ACT.Exp).then_inc(s["exp_done"], 1)
                    elif step in ("RZ", "V2", "V3"):
                        for m in (0, 1) if step == "RZ" else (int(step[1]),):
                            gate("scanned", 4 * i + m + 1)
                            gate("pj_filled", 16 * i)
                            act.activation(aT[0][:, m, :], att[:, m % 2, :], ACT.Copy).then_inc(s["a_hi"], 1)
                    if step[0] in "QKVO" and "." not in step:
                        used += 1
                    if "." not in step:
                        continue
                    slot, what = step.split(".")
                    n = SLOTS.index(slot)
                    j = JOBS * i + n
                    edge = slot[0] == "E"
                    R = ET if edge else P

                    def deviation(c):
                        gate(f"mv{c}_done", 2 * (j + 1))
                        gate(f"rs{c}_done", j)
                        act.activation(sd[c - 1][0:R, :], mv[c - 1][0:R, :, 1], ACT.Sqrt, bias=eps_col[0:R, :])\
                            .then_inc(s[f"sd{c}_done"], 1)

                    def normalize(c, dest, source, done):
                        gate(f"nm{c}_done", j + 1)
                        for t in range(2):
                            ins = act.activation(dest[0:R, t, :], source[0:R, t, :], ACT.Identity,
                                                 scale=rs[c - 1][0:R, t:t + 1], bias=nm[c - 1][0:R, t:t + 1])
                        ins.then_inc(s[done], 1)

                    if what == "sum1":
                        deviation(1)
                    elif what == "norm1":
                        gate("tr_filled", FILLS * i + fill)
                        gate("xr_done", j)
                        normalize(1, n1, n1 if edge else xin[n % 2], "n1_done")
                    elif what == "T":
                        for half in range(2):
                            gate("tr_filled", FILLS * i + fill + 1)
                            gate("h_filled", j)
                            act.activation(nT[0][:, 2 * half:2 * half + 2, 0:2 * R],
                                           pT[fill % 2][:, :].rearrange("p (a n) -> p a n", a=2)[:, :, 0:2 * R], ACT.Copy)\
                                .then_inc(s["tr_hi"], 1)
                            fill += 1
                    elif what == "F1":
                        gate("relu_done", j + 1)
                        gate("f_filled", 2 * j)
                        act.activation(hT[:, 0:2 * R], h_relu[:, 0:2 * R], ACT.Copy).then_inc(s["h_hi"], 1)
                    elif what == "F2":
                        deviation(2)
                    elif what == "norm2":
                        gate("mv3_done", 2 * j)
                        gate("z_rows", j)
                        normalize(2, y, x2, "n2_done")
                    elif what == "sum3":
                        deviation(3)
                    elif what == "norm3":
                        gate("out_edge", 64 * i + 32 * max(n - 4, 0))
                        gate("out_node", 128 * i + 32 * min(n, 4))
                        normalize(3, z, y, "z_rows")

            with act.Fori(0, ROUNDS) as i:
                one_round(i)

        @block.vector
        def _(dve):
            def gate(name, value):
                dve.wait_ge(s[name], value)
                dve.sem_inc(s["gate_dve"], 1)

            def by_head(ap, k):
                return ap[:, k, :].rearrange("p (h m d) -> p m h d", h=HEADS, m=KC)

            dve.wait_ge(s["idx_loaded"], 64)
            dve.tensor_copy(idx_f[0:CT, :, :], idx_raw[0:CT, :, :]).then_inc(s["idx_cast"], 1)
            turned = pZ[0:ET, 0:3 * CT].rearrange("p (a t) -> p a t", a=3)
            dve.wait_ge(s["idx_turned"], 1)
            dve.tensor_copy(src_idx[:, :], turned[:, 0, :]).then_inc(s["idx_done"], 1)
            dve.tensor_copy(dst_idx[:, :], turned[:, 1, :]).then_inc(s["idx_done"], 1)
            dve.tensor_copy(col_f[0:ET, :], turned[:, 2, :]).then_inc(s["last_flag"], 1)
            dve.wait_ge(s["last_flag"], 1)
            dve.tensor_tensor(part_f[0:ET, :], turned[:, 1, :], col_f[0:ET, :], ALU.is_equal).then_inc(s["last_flag"], 1)
            dve.wait_ge(s["last_flag"], 2)
            dve.scalar_tensor_tensor(last_idx[:, :], part_f[0:ET, :], float(SKIP), turned[:, 1, :], ALU.mult, ALU.add)\
                .then_inc(s["idx_done"], 1)

            splits = [0]

            def split_lo(w, stage, permute):
                for k in range(KC):
                    splits[0] += 1
                    dve.wait_ge(s["split_hi"], splits[0])
                    if permute:
                        view = lambda t: t[:, k, :].rearrange("p (m h d) -> p m h d", m=KC, h=HEADS)
                        for m in range(KC):
                            ins = dve.tensor_tensor(view(w[1])[:, m], by_head(stage, k)[:, m], view(w[0])[:, m].bitcast(F32), ALU.subtract)
                    else:
                        ins = dve.tensor_tensor(w[1][:, k, :], stage[:, k, :], w[0][:, k, :].bitcast(F32), ALU.subtract)
                    ins.then_inc(s["split_lo"], 1)

            dve.wait_ge(s["w1_loaded"], 80)
            for k in range(KC):
                dve.tensor_scalar(w1_scaled[:, k, :], w1_raw[:, k, :], g1_col[:, k:k + 1], None, ALU.mult).then_inc(s["w1_scale"], 1)
            split_lo(wq, w_stage["q"], True)
            dve.wait_ge(s["w1_hi"], 2)
            for half in range(2):
                dve.tensor_tensor(w1[1][:, :, DFF * half:DFF * half + DFF], w1_scaled,
                                  w1[0][:, :, DFF * half:DFF * half + DFF].bitcast(F32), ALU.subtract).then_inc(s["w1_lo"], 1)
            dve.wait_ge(s["w2_hi"], 1)
            dve.tensor_tensor(w2[1][:, :], w2_raw, w2[0][:, :].bitcast(F32), ALU.subtract).then_inc(s["w2_lo"], 1)
            dve.wait_ge(s["b1_folded"], 1)
            dve.tensor_tensor(b1_col[:, :], pF[0][:, 0:1], b1_col[:, :], ALU.add).then_inc(s["b1_done"], 1)
            dve.wait_ge(s["b_loaded"], 64)
            dve.wait_ge(s["zero_set"], 3)
            dve.tensor_tensor(b_sum, b_raw[:, 0, :], b_raw[:, 1, :], ALU.add).then_inc(s["bias_sum"], 1)
            dve.memset(ones[:, :].bitcast(F32), 1.0).then_inc(s["ones_set"], 1)
            split_lo(wk, w_stage["k"], True)
            dve.wait_ge(s["bias_hi"], 1)
            dve.tensor_tensor(bias2[32:33, :], b_sum[32:33, :], bias2[32:33, :].bitcast(F32), ALU.subtract).then_inc(s["bias_lo"], 1)

            dve.wait_ge(s["iota_set"], 2)
            dve.tensor_copy(iota_n, iota_i).then_inc(s["iota_cast"], 1)
            dve.wait_ge(s["idx_done"], 3)
            dve.tensor_scalar(part_i[0:ET, :], dst_idx[:, :], 1, P - 1, ALU.logical_shift_right, ALU.bitwise_and).then_inc(s["digit_low"], 1)
            dve.tensor_scalar(col_i[0:ET, :], dst_idx[:, :], 8, 1, ALU.logical_shift_right, ALU.logical_shift_left).then_inc(s["digit_low"], 1)
            dve.tensor_scalar(low_i[0:ET, :], dst_idx[:, :], 1, None, ALU.bitwise_and).then_inc(s["digit_low"], 1)
            dve.wait_ge(s["digit_low"], 3)
            dve.tensor_copy(part_f[0:ET, :], part_i[0:ET, :]).then_inc(s["digit_done"], 1)
            dve.tensor_tensor(col_f[0:ET, :], col_i[0:ET, :], low_i[0:ET, :], ALU.add).then_inc(s["digit_done"], 1)
            dve.wait_ge(s["digit_done"], 2)
            dve.wait_ge(s["iota_cast"], 1)
            for c in range(CT // OHT):
                if c:
                    dve.wait_ge(s["counted"], c)
                for oh, digit, width in ((oh_p, part_f, P), (oh_c, col_f, CN)):
                    dve.tensor_tensor(oh, iota_n[0:ET, 0:width].rearrange("p (a n) -> p a n", a=1).broadcast_to([ET, OHT, width]),
                                      digit[0:ET, OHT * c:OHT * c + OHT].rearrange("p (t a) -> p t a", a=1).broadcast_to([ET, OHT, width]),
                                      ALU.is_equal).then_inc(s["onehot"], 1)
            dve.wait_ge(s["counted"], CT // OHT)
            dve.tensor_scalar(has_edge, pS[:, 0:CN], 0.5, float(SKIP), ALU.is_gt, ALU.mult).then_inc(s["flag_done"], 1)
            dve.wait_ge(s["flag_done"], 1)
            dve.tensor_tensor(node_idx[:, :], has_edge, node_i, ALU.add).then_inc(s["node_done"], 1)
            split_lo(wv, w_stage["v"], True)
            split_lo(wo, w_stage["o"], False)
            for name in ("tr_hi", "tr_lo"):
                dve.sem_inc(s[name], 1)

            def one_round(i):
                fill = used = reads = 0
                for step in ROUND:
                    if step == "TXD":
                        gate("row_loaded", 16 * (i + 1))
                        gate("alpha_done", i)
                        dve.tensor_tensor(nsame[:, :], dst_row[:, 1:EG + 1], dst_row[:, 0:EG], ALU.is_equal).then_inc(s["mask_eq"], 1)
                    if step in ("TXD", "TXS"):
                        for k in range(KC):
                            gate("tr_hi", FILLS * i + fill + 2)
                            if step == "TXD":
                                gate("pj_filled", 16 * i)
                            else:
                                gate("pj_filled", 16 * i + 4)
                            dve.tensor_tensor(xT[1][:, k, :], pT[fill % 2][:, 0:EG], xT[0][:, k, :].bitcast(F32), ALU.subtract)\
                                .then_inc(s["tr_lo"], 1)
                            fill += 1
                    elif step[0] == "K":
                        m = int(step[1])
                        gate("pj_filled", 16 * i + used + 1)
                        gate("q_saved", 4 * i + m + 1)
                        if m == 0:
                            gate("score_done", i)
                        else:
                            gate("qk_acc", 3 * i + m - 1)
                        dve.tensor_tensor((qk if m == 0 else qk_m)[:, :], pP[used % 2][:, 0:EG], q[:, m, 0:EG], ALU.mult)\
                            .then_inc(s["qk_part"], 1)
                    elif step == "S":
                        gate("score_done", i + 1)
                        gate("mask_done", 2 * i + 2)
                        gate("max_carried", i)
                        dve.tensor_tensor_scan(mx[:, 1:EG + 1], far[:, :], pS[:, 0:EG], mx[:, 0:1], ALU.add, ALU.max)\
                            .then_inc(s["max_done"], 1)
                        gate("max_done", i + 1)
                        gate("alpha_done", i)
                        gate("scanned", 4 * i)
                        dve.tensor_tensor(ex[:, 1, :], pS[:, 0:EG], mx[:, 1:EG + 1], ALU.subtract).then_inc(s["weight_exp"], 1)
                        gate("exp_done", i + 1)
                        gate("z_carried", i)
                        gate("zT_done", i)
                        dve.tensor_tensor_scan(zs[:, 1:EG + 1], ex[:, 0, :], ex[:, 1, :], zs[:, 0:1], ALU.mult, ALU.add)\
                            .then_inc(s["z_done"], 1)
                        gate("z_done", i + 1)
                        dve.tensor_copy(zs[:, 0:1], zs[:, EG:EG + 1]).then_inc(s["z_carried"], 1)
                    elif step == "ZT":
                        gate("zT_done", i + 1)
                        dve.reciprocal(rz[:, :, :], pZ[0:ET, :].rearrange("p (t h d) -> p t h d", t=4, h=HEADS)[:, :, :, 0])\
                            .then_inc(s["rz_done"], 1)
                        gate("rz_done", i + 1)
                        gate("rzb_done", i)
                        dve.tensor_copy(rz_all[:, :, :].rearrange("p t (h d) -> p (t h) d", h=HEADS),
                                        rz[:, :, :].rearrange("p t (h a) -> p (t h) a", a=1).broadcast_to([ET, 4 * HEADS, HD]))\
                            .then_inc(s["rz_spread"], 1)
                    elif step == "RZ":
                        gate("rzb_done", i + 1)
                        dve.tensor_tensor(ex[:, 1, :], pS[:, 0:EG], ex[:, 1, :], ALU.mult).then_inc(s["beta_done"], 1)
                        gate("beta_done", i + 1)
                        dve.scalar_tensor_tensor(ex[:, 0, :], ex[:, 1, :], 1.0, nsame[:, :], ALU.subtract, ALU.mult)\
                            .then_inc(s["alpha_done"], 1)
                        for m in range(2):
                            weigh(i, m, m % 2)
                    elif step[0] == "V" and int(step[1]) >= 2:
                        weigh(i, int(step[1]), used % 2)
                    if step[0] in "QKVO" and "." not in step:
                        used += 1
                    if "." not in step:
                        continue
                    slot, what = step.split(".")
                    n = SLOTS.index(slot)
                    j = JOBS * i + n
                    edge = slot[0] == "E"
                    R = ET if edge else P

                    def moments(c, source):
                        for t in range(2):
                            dve.bn_stats(st[c - 1][0:R, t, :], source[0:R, t, :]).then_inc(s[f"st{c}_done"], 1)
                        for t in range(2):
                            gate(f"st{c}_done", 2 * j + t + 1)
                            dve.bn_aggr(mv[c - 1][0:R, t, :], st[c - 1][0:R, t, :]).then_inc(s[f"mv{c}_done"], 1)

                    def scales(c):
                        gate(f"sd{c}_done", j + 1)
                        gate(f"n1_done" if c == 1 else f"n2_done" if c == 2 else "z_rows", j)
                        dve.reciprocal(rs[c - 1][0:R, :], sd[c - 1][0:R, :]).then_inc(s[f"rs{c}_done"], 1)
                        gate(f"rs{c}_done", j + 1)
                        dve.scalar_tensor_tensor(nm[c - 1][0:R, :], mv[c - 1][0:R, :, 0], -1.0, rs[c - 1][0:R, :], ALU.mult, ALU.mult)\
                            .then_inc(s[f"nm{c}_done"], 1)

                    if what == "sum1":
                        if edge:
                            gate(f"erow_loaded{n % 2}", 32 * (i + 1))
                            gate("tr_filled", FILLS * i + fill)
                            gate("xr_done", j)
                            for t in range(2):
                                o = 2 * (n - 4) + t
                                gate("pj_filled", 16 * i + 12 + o + 1)
                                dve.tensor_tensor(n1[0:R, t, :], pP[o % 2][0:R, :], xin[n % 2][0:R, t, :], ALU.add)\
                                    .then_inc(s["hx_done"], 1)
                            gate("hx_done", 4 * i + 2 * (n - 4) + 2)
                            gate("nm1_done", j)
                            moments(1, n1)
                        else:
                            gate(f"xin_loaded{n % 2}", 16 * (2 * i + n // 2 + 1))
                            gate("nm1_done", j)
                            moments(1, xin[n % 2])
                    elif what == "norm1":
                        scales(1)
                    elif what == "T":
                        for half in range(2):
                            gate("tr_hi", FILLS * i + fill + 2)
                            gate("h_filled", j)
                            c = slice(2 * half, 2 * half + 2)
                            dve.tensor_tensor(nT[1][:, c, 0:2 * R], pT[fill % 2][:, :].rearrange("p (a n) -> p a n", a=2)[:, :, 0:2 * R],
                                              nT[0][:, c, 0:2 * R].bitcast(F32), ALU.subtract).then_inc(s["tr_lo"], 1)
                            fill += 1
                    elif what == "F1":
                        gate("h_filled", j + 1)
                        gate("h_lo", j)
                        dve.tensor_scalar(h_relu[:, 0:2 * R], pF[0][:, 0:2 * R], b1_col[:, 0:1], 0.0, ALU.add, ALU.max)\
                            .then_inc(s["relu_done"], 1)
                        gate("h_hi", j + 1)
                        dve.tensor_tensor(hT[DFF:P, 0:2 * R], h_relu[DFF:P, 0:2 * R], hT[DFF:P, 0:2 * R].bitcast(F32), ALU.subtract)\
                            .then_inc(s["h_lo"], 1)
                    elif what == "F2":
                        gate("xr_done", j + 1)
                        for t in range(2):
                            gate("f_filled", 2 * j + t + 1)
                            dve.tensor_tensor(x2[0:R, t, :], pF[(t + 1) % 2][0:R, :], x2[0:R, t, :], ALU.add).then_inc(s["x2_done"], 1)
                        gate("x2_done", 2 * j + 2)
                        gate("nm2_done", j)
                        moments(2, x2)
                    elif what == "norm2":
                        scales(2)
                    elif what == "sum3":
                        gate("s_done", j + 2)
                        gate("nm3_done", j)
                        moments(3, y)
                    elif what == "norm3":
                        scales(3)

            def weigh(i, m, bank):
                gate("pj_filled", 16 * i + 8 + m + 1)
                gate("beta_done", i + 1)
                gate("scanned", 4 * i + max(m - 1, 0))
                dve.tensor_tensor(wgt[:, m % 2, :], pP[bank][:, 0:EG], ex[:, 1, :], ALU.mult).then_inc(s["weighted"], 1)
                gate("weighted", 4 * i + m + 1)
                gate("alpha_done", i + 1)
                gate("a_lo", 4 * i + max(m - 1, 0))
                gate("carried", 4 * i)
                dve.tensor_tensor_scan(att[:, m % 2, :], ex[:, 0, :], wgt[:, m % 2, :], carry[:, m:m + 1], ALU.mult, ALU.add)\
                    .then_inc(s["scanned"], 1)
                gate("scanned", 4 * i + m + 1)
                dve.tensor_copy(carry[:, m:m + 1], att[:, m % 2, EG - 1:EG]).then_inc(s["carried"], 1)
                gate("a_hi", 4 * i + m + 1)
                gate("pj_filled", 16 * i)
                dve.tensor_tensor(aT[1][:, m, :], att[:, m % 2, :], aT[0][:, m, :].bitcast(F32), ALU.subtract)\
                    .then_inc(s["a_lo"], 1)

            with dve.Fori(0, ROUNDS) as i:
                one_round(i)

        @block.tensor
        def _(pe):
            pe.wait_ge(s["ident_done"], 1)
            pe.wait_ge(s["idx_cast"], 1)
            turned = pZ[0:ET, 0:3 * CT].rearrange("p (a t) -> p a t", a=3)
            for a in range(3):
                ins = pe.transpose(turned[:, a, :], idx_f[0:CT, a, :], ident[0:CT, 0:CT])
            ins.then_inc(s["idx_turned"], 1)
            pe.wait_ge(s["w1_loaded"], 80)
            for half in range(2):
                for k in range(KC):
                    ins = pe.matmul(pF[0][DFF * half:DFF * half + DFF, 0:1], w1_raw[:, k, :], be1_col[:, k:k + 1],
                                    start=(k == 0), stop=(k == KC - 1))
            ins.then_inc(s["b1_folded"], 1)
            for c in range(CT // OHT):
                pe.wait_ge(s["onehot"], 2 * c + 2)
                for t in range(OHT):
                    ins = pe.matmul(pS[:, 0:CN], oh_p[:, t, :], oh_c[:, t, :], start=(c + t == 0), stop=(c == CT // OHT - 1 and t == OHT - 1))
                ins.then_inc(s["counted"], 1)
            pe.wait_ge(s["head_done"], 1)
            pe.wait_ge(s["bias_lo"], 1)
            pe.wait_ge(s["ones_set"], 1)
            pe.wait_ge(s["b1_done"], 1)
            pe.wait_ge(s["w1_lo"], 2)
            pe.wait_ge(s["w2_lo"], 1)
            pe.wait_ge(s["node_done"], 1)
            pe.wait_ge(s["split_lo"], 4 * KC)

            def split_product(acc, left, right, n):
                for k in range(n):
                    for a, b in ((0, 0), (0, 1), (1, 0)):
                        ins = pe.matmul(acc, left(a, k), right(b, k), start=(k == 0 and a == b), stop=(k == n - 1 and a == 1))
                return ins

            def one_round(i):
                fill = used = reads = 0

                def bank_free():
                    pe.wait_ge(s["tr_lo"], FILLS * i + fill)

                for step in ROUND:
                    if step in ("TXD", "TXS"):
                        rows_in = xd if step == "TXD" else xs
                        pe.wait_ge(s["xd_loaded" if step == "TXD" else "xs_loaded"], 64 * (i + 1))
                        for k in range(KC):
                            bank_free()
                            for t in range(4):
                                ins = pe.transpose(pT[fill % 2][:, ET * t:ET * t + ET], rows_in[:, t, P * k:P * k + P], ident[0:ET, 0:ET])
                            ins.then_inc(s["tr_filled"], 1)
                            fill += 1
                        xT_fill = fill
                    elif "." not in step and step[0] in "QKV":
                        m = int(step[1])
                        w = {"Q": wq, "K": wk, "V": wv}[step[0]]
                        pe.wait_ge(s["tr_lo"], FILLS * i + xT_fill + 1)
                        free_bank(i, used)
                        split_product(pP[used % 2][:, 0:EG], lambda a, k: w[a][:, k, P * m:P * m + P], lambda b, k: xT[b][:, k, :], KC)\
                            .then_inc(s["pj_filled"], 1)
                        used += 1
                    elif step == "S":
                        pe.wait_ge(s["qk_acc"], 3 * i + 3)
                        pe.wait_ge(s["beta_done"], i)
                        pe.matmul(pS[:, 0:EG], same_head[:, :], qk[:, :], start=True, stop=True).then_inc(s["score_done"], 1)
                    elif step == "ZT":
                        pe.wait_ge(s["z_done"], i + 1)
                        for t in range(4):
                            ins = pe.transpose(pZ[0:ET, P * t:P * t + P], zs[:, 1 + ET * t:1 + ET * t + ET], ident[:, :])
                        ins.then_inc(s["zT_done"], 1)
                    elif step == "RZ":
                        pe.wait_ge(s["rz_spread"], i + 1)
                        pe.wait_ge(s["weight_exp"], i + 1)
                        for t in range(4):
                            ins = pe.transpose(pS[:, ET * t:ET * t + ET], rz_all[:, t, :], ident[0:ET, 0:ET])
                        ins.then_inc(s["rzb_done"], 1)
                    elif "." not in step and step[0] == "O":
                        t = int(step[1])
                        pe.wait_ge(s["a_lo"], 4 * i + 4)
                        free_bank(i, used)
                        split_product(pP[used % 2][0:ET, :], lambda a, m: aT[a][:, m, ET * t:ET * t + ET], lambda b, m: wo[b][:, m, :], KC)\
                            .then_inc(s["pj_filled"], 1)
                        used += 1
                    if "." not in step:
                        continue
                    slot, what = step.split(".")
                    n = SLOTS.index(slot)
                    j = JOBS * i + n
                    edge = slot[0] == "E"
                    R = ET if edge else P
                    if what == "T":
                        pe.wait_ge(s["n1_done"], j + 1)
                        for half in range(2):
                            bank_free()
                            for c in range(2):
                                k = 2 * half + c
                                for t in range(2):
                                    ins = pe.transpose(pT[fill % 2][:, NB * c + R * t:NB * c + R * t + R], n1[0:R, t, P * k:P * k + P], ident[0:R, 0:R])
                            ins.then_inc(s["tr_filled"], 1)
                            fill += 1
                        nT_fill = fill
                    elif what == "F1":
                        pe.wait_ge(s["tr_lo"], FILLS * i + fill_of[slot] + 1)
                        pe.wait_ge(s["x2_done"], 2 * j)
                        split_product(pF[0][:, 0:2 * R], lambda a, k: w1[a][:, k, :], lambda b, k: nT[b][:, k, 0:2 * R], KC)\
                            .then_inc(s["h_filled"], 1)
                    elif what == "F2":
                        pe.wait_ge(s["h_lo"], j + 1)
                        for t in range(2):
                            f = pF[(t + 1) % 2][0:R, :]
                            if t == 0:
                                pe.wait_ge(s["x2_done"], 2 * j)
                            pe.matmul(f, hT[:, R * t:R * t + R], w2[0][:, :], start=True, stop=False)
                            pe.matmul(f, hT[:, R * t:R * t + R], w2[1][:, :], start=False, stop=False)
                            pe.matmul(f, ones[:, 0:R], bias2[:, :], start=False, stop=True).then_inc(s["f_filled"], 1)

            fill_of, fills = {}, 0
            for step in ROUND:
                fills += 4 if step in ("TXD", "TXS") else 2 if step.endswith(".T") else 0
                fill_of[step.split(".")[0]] = fills if step.endswith(".T") else fill_of.get(step.split(".")[0], 0)

            def free_bank(i, used):
                if used < 2:
                    pe.wait_ge(s["hx_done"], 4 * i)
                elif used < 6:
                    pe.wait_ge(s["q_saved"], 4 * i + used - 1)
                elif used < 10:
                    pe.wait_ge(s["qk_part"], 4 * i + used - 5)
                elif used < 14:
                    pe.wait_ge(s["weighted"], 4 * i + used - 9)
                else:
                    pe.wait_ge(s["hx_done"], 4 * i + used - 13)

            with pe.Fori(0, ROUNDS) as i:
                one_round(i)


_INS = ["x", "src", "dst", "L0_gnn_Wq", "L0_gnn_Wk", "L0_gnn_Wv", "L0_gnn_Wo", "L0_gnn_ln1_g", "L0_gnn_ln1_b",
        "L0_gnn_ln2_g", "L0_gnn_ln2_b", "L0_gnn_W1", "L0_gnn_b1", "L0_gnn_W2", "L0_gnn_b2"]


def kernel(**inputs):
    import numpy as _np
    import concourse.bacc as _bacc
    from concourse import mybir as _mybir
    from concourse.bass_utils import run_bass_kernel_spmd as _run

    nc = _bacc.Bacc("TRN2", target_bir_lowering=False, num_devices=1)
    arrays, args = {}, []
    for name in _INS:
        a = _np.ascontiguousarray(inputs[name])
        arrays[f"in_{name}_dram"] = a
        args.append(nc.dram_tensor(f"in_{name}_dram", a.shape, _mybir.dt.from_np(a.dtype), kind="ExternalInput").ap())
    out = nc.dram_tensor("out_0_dram", inputs["x"].shape, _mybir.dt.float32, kind="ExternalOutput").ap()
    graph_attention(nc, *args, out)
    r = _run(nc, [arrays], core_ids=[0])
    return r.results[0]["out_0_dram"]
```

```python
from contextlib import ExitStack

import concourse.bass as bass
from concourse import mybir

F32 = mybir.dt.float32
F32R = mybir.dt.float32r
BF16 = mybir.dt.bfloat16
I32 = mybir.dt.int32
U32 = mybir.dt.uint32
ALU = mybir.AluOpType
ACT = mybir.ActivationFunctionType

HEADS = 8
EPS = 1e-5
SKIP = 1 << 20
FAR = 3.0e38

ORDER = {
    "pe": """
E1.F1- TXD0 TXD1 E1.F2- TXD2 TXD3 A.T Q0 TXS0 A.F1 Q1 A.F2 Q2 Q3 TXS1 TXS2 TXS3 B.T K0 B.F1 K1 K2
B.F2 K3 C.T S V0 C.F1 ZT C.F2 RZ V1 D.T V2 D.F1 V3 D.F2 O0 O1 O2 O3 E0.T E0.F1 E1.T E0.F2
""".split(),
    "act": """
E0.T- E1.sd- E0.F1- E1.T- E0.sq- E1.F1- TXD0 TXD1 A.sd E0.sq3- TXD2 TXD3 E1.sq- A.T Q0 E1.sq3- A.F1
B.sd Q1 A.sq TXS0 TXS1 Q2 TXS2 TXS3 C.sd B.T A.sq3 Q3 B.F1 D.sd B.sq C.T B.sq3 S C.F1 V0 D.T V1 C.sq
V2 V3 D.F1 C.sq3 D.sq E0.sd D.sq3
""".split(),
    "dve": """
D.t- E0.sum1- D.norm2- E0.norm1- E1.sum1- E1.norm1- D.norm3- A.sum1 E0.x2- E0.t- E0.norm2- TXD0
E1.x2- TXD1 A.norm1 TXD2 TXD3 E0.norm3- TXD E1.t- E1.norm2- B.sum1 E1.norm3- B.norm1 A.x2 C.sum1 A.t
A.norm2 TXS0 TXS1 TXS2 TXS3 A.norm3 K0 C.norm1 D.sum1 K1 K2 B.x2 B.t K3 D.norm1 B.norm2 S B.norm3 ZT
C.x2 RZ V0 C.t V1 V2 V3 C.norm2 D.x2 C.norm3
""".split(),
    "pool": """
D.xr- B.out- C.out- E0.xb- E1.xb- E0.xr- GXD- D.out- E1.xr- A.xb E0.out- A.xr E1.out- TXD B.xb C.xb
B.xr K1 A.out K2 K3 S C.xr GXS D.xb
""".split(),
}
SLOTS = ["A", "B", "C", "D", "E0", "E1"]
JOBS = len(SLOTS)
FILLS = 4 + 4 + 2 * JOBS


def graph_attention(nc, x, src, dst, Wq, Wk, Wv, Wo, g1, be1, g2, be2, W1, b1, W2, b2, out):
    N, D = x.shape
    E = src.shape[0]
    DFF = W1.shape[1]
    P = 128
    KC = D // P
    HD = P // HEADS
    DK = D // HEADS
    ET = 125
    EG = KC * ET
    ROUNDS = E // EG
    NB = 2 * P
    TAIL = (N - (4 * ROUNDS - 1) * NB) // 2
    CT = E // ET
    CN = 8 * ROUNDS
    assert E == ROUNDS * EG and N <= 4 * ROUNDS * NB and TAIL > 0 and D == 512 and 2 * DFF == P

    ctx = ExitStack()
    with ctx:
        def sb(name, shape, dt=F32):
            return ctx.enter_context(nc.sbuf_tensor(name, shape, dt))

        def sem(name):
            return ctx.enter_context(nc.semaphore(name))

        ident = sb("ident", [P, P])
        same_head = sb("same_head", [P, P])
        wq = [sb(f"wq_{n}", [P, KC, D], F32R) for n in ("hi", "lo")]
        wk = [sb(f"wk_{n}", [P, KC, D], F32R) for n in ("hi", "lo")]
        wv = [sb(f"wv_{n}", [P, KC, D], F32R) for n in ("hi", "lo")]
        wo = [sb(f"wo_{n}", [P, KC, D], F32R) for n in ("hi", "lo")]
        w1 = sb("w1", [P, KC, DFF])
        w2 = sb("w2", [DFF + 1, D])
        g1_all = sb("g1_all", [P, D])
        g2_all = sb("g2_all", [P, D])
        be2_all = sb("be2_all", [P, D])
        g1_col = sb("g1_col", [P, KC])
        be1_col = sb("be1_col", [P, KC])
        b1_col = sb("b1_col", [DFF, 1])
        eps_col = sb("eps_col", [P, 1])
        src_idx = sb("src_idx", [ET, CT], I32)
        dst_idx = sb("dst_idx", [ET, CT], I32)
        last_idx = sb("last_idx", [ET, CT], I32)
        node_idx = sb("node_idx", [P, CN], I32)
        src_now = sb("src_now", [ET, 4], I32)
        dst_now = sb("dst_now", [ET, 4], I32)
        last_now = sb("last_now", [ET, 4], I32)
        node_now = sb("node_now", [P, 8], I32)
        xs = sb("xs", [ET, 4, D])
        xd = sb("xd", [ET, 4, D])
        xT = [sb(f"xT_{n}", [P, KC, EG], F32R) for n in ("hi", "lo")]
        q = sb("q", [P, KC, D])
        qk = sb("qk", [P, EG])
        qk_m = sb("qk_m", [P, EG])
        dst_row = sb("dst_row", [P, EG + 1], I32)
        far = sb("far", [P, EG])
        nsame = sb("nsame", [P, EG])
        mx = sb("mx", [P, EG + 1])
        zs = sb("zs", [P, EG + 1])
        ex = sb("ex", [P, 2, EG])
        rz = sb("rz", [ET, 4, HEADS])
        rz_all = q[0:ET, 0, :].rearrange("p (t n) -> p t n", t=4)
        wgt = sb("wgt", [P, 2, EG])
        att = sb("att", [P, 2, EG])
        carry = sb("carry", [P, KC])
        aT = [sb(f"aT_{n}", [P, KC, EG], F32R) for n in ("hi", "lo")]
        xin = [sb(f"xin{n}", [P, 2, D]) for n in range(2)]
        xb = [sb(f"xb{n}", [P, 2, D]) for n in range(2)]
        rows = sb("rows", [P, 12, D])
        n1 = [rows[:, 2 * n:2 * n + 2, :] for n in (0, 2)]
        x2 = [rows[:, 2 * n:2 * n + 2, :] for n in (1, 3)]
        y = [rows[:, 2 * n:2 * n + 2, :] for n in (4, 5)]
        squares = [None] + [sb(f"squares{n}", [P, 2, D], BF16) for n in (2, 3)]
        nT = sb("nT", [P, KC, NB])
        hT = sb("hT", [DFF + 1, NB])
        st = sb("st", [P, 2, 6])
        mv = [sb(f"mv{n}", [P, 2, 2]) for n in range(2)]
        sums = [None] + [sb(f"sums{n}", [P, 2]) for n in (2, 3)]
        sq = [None] + [sb(f"sq{n}", [P, 2]) for n in (2, 3)]
        nmean = [None] + [[sb(f"nmean{c}_{n}", [P, 2]) for n in range(2)] for c in (2, 3)]
        sd = [[sb(f"sd{c}_{n}", [P, 2]) for n in range(2)] for c in (1, 2, 3)]
        rs = [[sb(f"rs{c}_{n}", [P, 2]) for n in range(2)] for c in (1, 2, 3)]

        pT = [ctx.enter_context(nc.psum_tensor(f"pT{n}", [P, 512], F32)) for n in range(2)]
        pP = [ctx.enter_context(nc.psum_tensor(f"pP{n}", [P, 512], F32)) for n in range(3)]
        pS = ctx.enter_context(nc.psum_tensor("pS", [P, 512], F32))
        pF = [ctx.enter_context(nc.psum_tensor(f"pF{n}", [P, 512], F32)) for n in range(2)]

        w_stage = {"q": q[:, :, :], "k": rows[:, 0:4, :], "o": rows[:, 4:8, :], "v": q[:, :, :]}
        w1_raw = xin[0][:, 0, 0:KC * DFF].rearrange("p (k f) -> p k f", k=KC)
        be1_row = xb[1][DFF:DFF + 1, 0, :]
        idx_raw = ex[:, :, :].rearrange("p a b -> p (a b)")[:, 0:3 * ET].bitcast(I32).rearrange("p (a b) -> p a b", a=3)
        idx_f = ex[:, :, :].rearrange("p a b -> p (a b)")[:, 512:512 + 3 * ET].rearrange("p (a b) -> p a b", a=3)
        OHT = 10
        oh_p = att[:, :, :].rearrange("p a b -> p (a b)").bitcast(BF16)[0:ET, 0:OHT * P].rearrange("p (t n) -> p t n", t=OHT)
        oh_c = wgt[:, :, :].rearrange("p a b -> p (a b)").bitcast(BF16)[0:ET, 0:OHT * CN].rearrange("p (t n) -> p t n", t=OHT)
        iota_n = qk[:, 0:P]
        iota_i = qk_m[:, 0:P].bitcast(I32)
        node_i = qk_m[:, P:P + CN].bitcast(I32)
        part_i = qk[:, P:P + CT].bitcast(I32)
        col_i = qk[:, 2 * P:2 * P + CT].bitcast(I32)
        low_i = qk[:, 3 * P:3 * P + CT].bitcast(I32)
        part_f = qk_m[:, 2 * P:2 * P + CT]
        col_f = qk_m[:, 2 * P + CT:2 * P + 2 * CT]
        has_edge = qk_m[:, 3 * P:3 * P + CN]

        names = """idx_loaded wq_loaded wk_loaded wv_loaded wo_loaded w1_loaded w2_loaded all_loaded
        row_loaded ident_set ident_done head_set head_done zero_set idx_cast idx_turned idx_done last_flag
        split_hi split_lo w1_done w2_done b1_folded b1_done ones_set
        iota_set iota_cast digit_low digit_col digit_done onehot counted flag_done node_done init_done
        gate_sp gate_pool gate_act gate_dve
        src_picked dst_picked last_picked node_picked xs_loaded xd_loaded xin_loaded0 xin_loaded1
        mask_eq mask_done
        tr_filled xT_hi xT_lo nT_done pj_filled q_saved qk_part qk_acc qk_done score_done max_done max_carried
        decay_half decay_done weight_exp exp_done z_done z_carried zT_done rz_done rz_spread rzb_done beta_done alpha_done
        weighted scanned carried a_hi a_lo
        hx_done st1_done mv1_done sd1_done rs1_done n1_done xb_done xr_done
        h_filled h_done f_filled x2_done nm2_done sq2_done sd2_done rs2_done t_done
        y_done nm3_done sq3_done sd3_done rs3_done z_rows out_A out_B out_C out_D out_E0 out_E1""".split()
        s = {name: sem(name) for name in names}

        FILL, END, fills = {}, {}, 0
        pe_steps = [step for step in ORDER["pe"] if not step.endswith("-")] + [step[:-1] for step in ORDER["pe"] if step.endswith("-")]
        for step in pe_steps:
            if step[:2] == "TX" or step.endswith(".T"):
                FILL[step] = fills
                fills += 2 if step.endswith(".T") else 1
                END[step] = fills
        PLACE = {f"{kind}{m}": 4 * n + m for n, kind in enumerate("QKVO") for m in range(4)}
        BANK = [n % 3 for n in range(15)] + [1]

        def bank(step):
            return pP[BANK[PLACE[step]]]


        def run(engine, order, one_step, keep_last=False):
            late = [step for step in order if step.endswith("-")]
            first, end = 0, ROUNDS - (1 if keep_last else 0)

            def one_round(i):
                for step in order:
                    if step.endswith("-"):
                        if not isinstance(i, int) or i > 0:
                            one_step(i - 1, step[:-1])
                    else:
                        one_step(i, step)

            if late:
                one_round(0)
                first = 1
            with engine.Fori(first, end) as i:
                one_round(i)
            if keep_last:
                one_round(ROUNDS - 1)
            for step in late:
                one_step(ROUNDS - 1, step[:-1])

        block = ctx.enter_context(nc.Block())

        def bcast_rows(ap, n):
            return bass.AP(tensor=ap.tensor, offset=ap.offset, ap=[[0, P], [1, n]])

        @block.sync
        def _(sp):
            def gate(name, value):
                sp.wait_ge(s[name], value)
                sp.sem_inc(s["gate_sp"], 1)

            def rows_of(block_no, parts=P):
                return x[bass.ds(NB * block_no, 2 * parts), :].rearrange("(p t) d -> p t d", t=2)

            def load_dst_row(i):
                sp.dma_start(dst_row[:, :], bass.AP(tensor=dst.tensor, offset=dst.offset + (EG * i - 1), ap=[[0, P], [1, EG + 1]]))\
                    .then_inc(s["row_loaded"], 16)

            sp.dma_start(idx_raw[0:CT, 0, :], src.rearrange("(t e) -> t e", e=ET)).then_inc(s["idx_loaded"], 16)
            sp.dma_start(idx_raw[0:CT, 1, :], dst.rearrange("(t e) -> t e", e=ET)).then_inc(s["idx_loaded"], 16)
            sp.wait_ge(s["zero_set"], 2)
            sp.dma_start(idx_raw[0:CT - 1, 2, :], dst[1:1 + (CT - 1) * ET].rearrange("(t e) -> t e", e=ET))\
                .then_inc(s["idx_loaded"], 16)
            sp.dma_start(idx_raw[CT - 1:CT, 2, 0:ET - 1], dst[1 + (CT - 1) * ET:E].rearrange("(t e) -> t e", t=1))\
                .then_inc(s["idx_loaded"], 16)
            sp.dma_start(w_stage["q"], Wq.rearrange("(k p) n -> p k n", p=P)).then_inc(s["wq_loaded"], 16)
            with nc.allow_non_contiguous_dma("short columns, once"):
                sp.dma_start(g1_col[:, :], g1.rearrange("(k p) -> p k", p=P)).then_inc(s["w1_loaded"], 16)
                sp.dma_start(be1_col[:, :], be1.rearrange("(k p) -> p k", p=P)).then_inc(s["w1_loaded"], 16)
                sp.dma_start(b1_col[:, :], b1.rearrange("(f a) -> f a", a=1)).then_inc(s["w1_loaded"], 16)
            sp.dma_start(w1_raw, W1.rearrange("(k p) f -> p k f", p=P)).then_inc(s["w1_loaded"], 16)
            sp.dma_start(w2[0:DFF, :], W2).then_inc(s["w2_loaded"], 16)
            sp.dma_start(w2[DFF:DFF + 1, :], b2.rearrange("(a n) -> a n", a=1)).then_inc(s["w2_loaded"], 16)
            sp.dma_start(be1_row, be1.rearrange("(a n) -> a n", a=1)).then_inc(s["w2_loaded"], 16)
            sp.dma_start(dst_row[:, 1:EG + 1], bcast_rows(dst, EG)).then_inc(s["row_loaded"], 16)
            sp.dma_start(w_stage["k"], Wk.rearrange("(k p) n -> p k n", p=P)).then_inc(s["wk_loaded"], 16)
            for tile, vec in ((g1_all, g1), (be2_all, be2), (g2_all, g2)):
                sp.dma_start(tile[:, :], bcast_rows(vec, D)).then_inc(s["all_loaded"], 16)
            wo_rows = Wo.rearrange("(h m d) n -> h d m n", h=HEADS, m=KC)
            for h in range(HEADS):
                sp.dma_start(w_stage["o"][HD * h:HD * h + HD, :, :], wo_rows[h]).then_inc(s["wo_loaded"], 16)
            sp.wait_ge(s["split_lo"], KC)
            sp.dma_start(w_stage["v"], Wv.rearrange("(k p) n -> p k n", p=P)).then_inc(s["wv_loaded"], 16)
            sp.wait_ge(s["b1_folded"], 1)
            sp.wait_ge(s["w1_done"], KC)
            for n in range(2):
                sp.dma_start(xin[n][:, :, :], rows_of(n)).then_inc(s[f"xin_loaded{n}"], 16)

            def round_loads(i, last):
                def load(n, block_no, parts=P):
                    gate("n1_done", JOBS * i + n + 2)
                    gate("xb_done", JOBS * i + n + 1)
                    sp.dma_start(xin[n % 2][0:parts, :, :], rows_of(block_no, parts)).then_inc(s[f"xin_loaded{n % 2}"], 16)

                load(0, 4 * i + 2)
                load(1, 4 * i + 3, TAIL if last else P)
                if last:
                    return
                gate("mask_eq", i + 1)
                load_dst_row(i + 1)
                load(2, 4 * i + 4)
                load(3, 4 * i + 5)

            with sp.Fori(0, ROUNDS - 1) as i:
                round_loads(i, last=False)
            round_loads(ROUNDS - 1, last=True)

        @block.gpsimd
        def _(pool):
            def gate(name, value):
                pool.wait_ge(s[name], value)
                pool.sem_inc(s["gate_pool"], 1)

            pool.memset(idx_raw[0:64, 2, :], -1).then_inc(s["zero_set"], 1)
            pool.memset(dst_row[:, 0:1], -1).then_inc(s["zero_set"], 1)
            pool.memset(ident[:, :], 0.0).then_inc(s["ident_set"], 1)
            pool.memset(same_head[:, :], DK ** -0.5).then_inc(s["head_set"], 1)
            pool.wait_ge(s["ident_set"], 1)
            pool.affine_select(out=ident[:, :], in_=ident[:, :], compare_op=ALU.not_equal, fill=1.0, base=0,
                               pattern=[[-1, P]], channel_multiplier=1).then_inc(s["ident_done"], 1)
            heads = same_head[:, :].rearrange("p (h d) -> p h d", h=HEADS)
            pool.wait_ge(s["head_set"], 1)
            pool.affine_select(out=heads, in_=heads, compare_op=ALU.is_ge, fill=0.0, base=0,
                               pattern=[[-HD, HEADS], [0, HD]], channel_multiplier=1).then_inc(s["head_set"], 1)
            pool.wait_ge(s["head_set"], 2)
            pool.affine_select(out=heads, in_=heads, compare_op=ALU.is_ge, fill=0.0, base=HD - 1,
                               pattern=[[HD, HEADS], [0, HD]], channel_multiplier=-1).then_inc(s["head_done"], 1)
            pool.iota(iota_i, pattern=[[1, P]], base=0, channel_multiplier=0).then_inc(s["iota_set"], 1)
            pool.iota(node_i.rearrange("p (b t) -> p b t", t=2), pattern=[[NB, CN // 2], [1, 2]], base=0,
                      channel_multiplier=2).then_inc(s["iota_set"], 1)
            pool.memset(eps_col[:, :], EPS).then_inc(s["init_done"], 1)
            pool.memset(mx[:, 0:1], 0.0).then_inc(s["init_done"], 1)
            pool.memset(zs[:, 0:1], 0.0).then_inc(s["init_done"], 1)
            pool.memset(carry[:, :], 0.0).then_inc(s["init_done"], 1)

            def pick(now, table, name, i, width, *free):
                for last_use in free:
                    gate(*last_use)
                pool.tensor_copy(now[:, :], table[:, bass.ds(width * i, width)]).then_inc(s[name], 1)

            def gather(dest, index, name):
                pool.indirect_dma_start(dest, None, x, bass.IndirectOffsetOnAxis(ap=index.bitcast(U32), axis=0),
                                        bounds_check=N - 1, oob_is_err=False).then_inc(s[name], 16)

            def scatter(rows_ap, index, name):
                pool.indirect_dma_start(out, bass.IndirectOffsetOnAxis(ap=index.bitcast(U32), axis=0), rows_ap, None,
                                        bounds_check=N - 1, oob_is_err=False).then_inc(s[name], 16)

            def gather_group(which, i, first):
                now, table, rows_in, end = {"dst": (dst_now, dst_idx, xd, END["TXD3"]), "src": (src_now, src_idx, xs, END["TXS3"])}[which]
                loaded = "xd_loaded" if which == "dst" else "xs_loaded"
                pick(now, table, f"{which}_picked", i, 4, *([] if first else [(loaded, 64 * i)]))
                gate(f"{which}_picked", i + 1)
                if not first:
                    gate("tr_filled", FILLS * (i - 1) + end)
                    if which == "dst":
                        gate("hx_done", 4 * i)
                        gate("xb_done", JOBS * i)
                for t in range(4):
                    gather(rows_in[:, t, :], now[:, t:t + 1], loaded)

            pool.wait_ge(s["idx_done"], 3)
            gather_group("dst", 0, first=True)
            gather_group("src", 0, first=True)

            def one_step(i, step):
                last = isinstance(i, int) and i == ROUNDS - 1
                if True:
                    def masks():
                        gate("mask_eq", i + 1)
                        gate("decay_done", i)
                        pool.tensor_scalar(far[:, :], nsame[:, :], FAR, -FAR, ALU.mult, ALU.add).then_inc(s["mask_done"], 1)
                        gate("mask_done", 2 * i + 1)
                        pool.tensor_scalar(nsame[:, :], nsame[:, :], -1.0, 0.0, ALU.mult, ALU.add).then_inc(s["mask_done"], 1)

                    if step == "TXD":
                        masks()
                        pick(last_now, last_idx, "last_picked", i, 4, ("out_E0", 32 * i), ("out_E1", 32 * i))
                        if isinstance(i, int) and i == 0:
                            pool.wait_ge(s["node_done"], 1)
                        pick(node_now, node_idx, "node_picked", i, 8, *[(f"out_{block_slot}", 32 * i) for block_slot in "ABCD"])
                    elif step[0] == "K" and step != "K0":
                        m = int(step[1])
                        gate("qk_part", 4 * i + m + 1)
                        if m > 1:
                            gate("qk_acc", 3 * i + m - 1)
                        pool.tensor_tensor(qk[:, :], qk[:, :], qk_m[:, :], ALU.add).then_inc(s["qk_acc"], 1)
                    elif step == "S":
                        gate("mask_done", 2 * i + 2)
                        gate("max_done", i + 1)
                        gate("scanned", 4 * i)
                        pool.tensor_tensor(ex[:, 0, :], mx[:, 0:EG], far[:, :], ALU.add).then_inc(s["decay_half"], 1)
                        gate("decay_half", i + 1)
                        pool.tensor_tensor(ex[:, 0, :], ex[:, 0, :], mx[:, 1:EG + 1], ALU.subtract).then_inc(s["decay_done"], 1)
                        gate("decay_done", i + 1)
                        gate("weight_exp", i + 1)
                        pool.tensor_copy(mx[:, 0:1], mx[:, EG:EG + 1]).then_inc(s["max_carried"], 1)
                    elif step in ("GXS", "GXD") and not last:
                        gather_group("src" if step == "GXS" else "dst", i + 1, first=False)
                    if "." not in step:
                        return
                    slot, what = step.split(".")
                    n = SLOTS.index(slot)
                    j = JOBS * i + n
                    edge = slot[0] == "E"
                    R = ET if edge else P
                    if what == "xb":
                        if not edge:
                            gate(f"xin_loaded{n % 2}", 16 * (2 * i + n // 2 + 1))
                        source = xd[:, 2 * n - 8:2 * n - 6, :] if edge else xin[n % 2]
                        gate("y_done", j)
                        pool.tensor_tensor(xb[n % 2][0:R, :, :], source[0:R, :, :],
                                           be2_all[0:R, :].rearrange("p (a d) -> p a d", a=1).broadcast_to([R, 2, D]), ALU.add)\
                            .then_inc(s["xb_done"], 1)
                    elif what == "xr":
                        gate("n1_done", j + 2)
                        gate("t_done", j)
                        gate("sq2_done", j)
                        pool.tensor_tensor(x2[n % 2][0:R, :, :], n1[n % 2][0:R, :, :],
                                           g1_all[0:R, :].rearrange("p (a d) -> p a d", a=1).broadcast_to([R, 2, D]), ALU.mult)\
                            .then_inc(s["xr_done"], 1)
                    elif what == "out":
                        gate("z_rows", j + 2)
                        gate("last_picked" if edge else "node_picked", i + 1)
                        for t in range(2):
                            if edge:
                                scatter(y[n % 2][0:R, t, :], last_now[:, 2 * (n - 4) + t:2 * (n - 4) + t + 1], f"out_{slot}")
                            else:
                                scatter(y[n % 2][0:R, t, :], node_now[:, 2 * n + t:2 * n + t + 1], f"out_{slot}")

            pool.wait_ge(s["all_loaded"], 48)
            pool.wait_ge(s["node_done"], 1)
            pool.sem_inc(s["xr_done"], 1)
            run(pool, ORDER["pool"], one_step, keep_last=True)
            for slot in SLOTS:
                pool.wait_ge(s[f"out_{slot}"], 32 * ROUNDS)

        @block.scalar
        def _(act):
            def gate(name, value):
                act.wait_ge(s[name], value)
                act.sem_inc(s["gate_act"], 1)

            def by_head(ap, k):
                return ap[:, k, :].rearrange("p (h m d) -> p m h d", h=HEADS, m=KC)

            def split_hi(w, stage, loaded, permute):
                act.wait_ge(s[loaded], 16 if loaded != "wo_loaded" else 16 * HEADS)
                for k in range(KC):
                    dest = w[0][:, k, :]
                    if permute:
                        act.activation(dest.rearrange("p (m h d) -> p m h d", m=KC, h=HEADS), by_head(stage, k), ACT.Copy)\
                            .then_inc(s["split_hi"], 1)
                    else:
                        act.activation(dest, stage[:, k, :], ACT.Copy).then_inc(s["split_hi"], 1)

            act.preload_act_table(ACT.Sqrt)
            split_hi(wq, w_stage["q"], "wq_loaded", True)
            split_hi(wk, w_stage["k"], "wk_loaded", True)
            split_hi(wv, w_stage["v"], "wv_loaded", True)
            split_hi(wo, w_stage["o"], "wo_loaded", False)
            act.wait_ge(s["init_done"], 4)

            def one_step(i, step):
                if True:
                    if step[:2] == "TX":
                        gate("tr_filled", FILLS * i + FILL[step] + 1)
                        if step[:3] == "TXD":
                            gate("pj_filled", 16 * i)
                        else:
                            gate("pj_filled", 16 * i + 4)
                        act.activation(xT[0][:, int(step[3]), :], pT[FILL[step] % 2][:, 0:EG], ACT.Copy).then_inc(s["xT_hi"], 1)
                    elif step[0] == "Q":
                        m = int(step[1])
                        gate("pj_filled", 16 * i + m + 1)
                        gate("rzb_done", i)
                        act.activation(q[:, m, 0:EG], bank(step)[:, 0:EG], ACT.Copy).then_inc(s["q_saved"], 1)
                    elif step == "S":
                        act.preload_act_table(ACT.Exp)
                        gate("decay_done", i + 1)
                        gate("weight_exp", i + 1)
                        act.activation(ex[:, :, :], ex[:, :, :], ACT.Exp).then_inc(s["exp_done"], 1)
                        act.preload_act_table(ACT.Sqrt)
                    elif step[0] == "V":
                        m = int(step[1])
                        gate("scanned", 4 * i + m + 1)
                        gate("pj_filled", 16 * i)
                        act.activation(aT[0][:, m, :], att[:, m % 2, :], ACT.Copy).then_inc(s["a_hi"], 1)
                    if "." not in step:
                        return
                    slot, what = step.split(".")
                    n = SLOTS.index(slot)
                    j = JOBS * i + n
                    edge = slot[0] == "E"
                    R = ET if edge else P

                    def deviation(c, var, scale):
                        gate(f"rs{c}_done", j)
                        act.activation(sd[c - 1][n % 2][0:R, :], var, ACT.Sqrt, bias=eps_col[0:R, :], scale=scale)\
                            .then_inc(s[f"sd{c}_done"], 1)

                    def squares_of(c, source):
                        gate(f"nm{c}_done", j + 1)
                        gate(f"sd{c}_done", j + 1)
                        for t in range(2):
                            ins = act.activation(squares[c - 1][0:R, t, :], source[0:R, t, :], ACT.Square,
                                                 bias=nmean[c - 1][n % 2][0:R, t:t + 1], accum_out=sq[c - 1][0:R, t:t + 1])
                        ins.then_inc(s[f"sq{c}_done"], 1)
                        gate(f"sq{c}_done", j + 1 + (c == 2))
                        deviation(c, sq[c - 1][0:R, :], 1.0 / D)

                    if what == "sd":
                        gate("mv1_done", 2 * j + 2)
                        deviation(1, mv[n % 2][0:R, :, 1], 1.0)
                    elif what == "T":
                        for half in range(2):
                            fill = FILL[step] + half
                            gate("tr_filled", FILLS * i + fill + 1)
                            gate("h_filled", j + 1)
                            act.activation(nT[:, 2 * half:2 * half + 2, 0:2 * R],
                                           pT[fill % 2][:, :].rearrange("p (a n) -> p a n", a=2)[:, :, 0:2 * R], ACT.Copy)\
                                .then_inc(s["nT_done"], 1)
                    elif what == "F1":
                        gate("h_filled", j + 2)
                        gate("f_filled", 2 * j)
                        act.activation(hT[0:DFF, 0:2 * R], pF[0][0:DFF, 0:2 * R], ACT.Relu, bias=b1_col[:, :]).then_inc(s["h_done"], 1)
                    elif what == "sq":
                        gate("sq2_done", j + 1)
                        squares_of(2, x2[n % 2])
                    elif what == "sq3":
                        gate("sq3_done", j)
                        squares_of(3, y[n % 2])

            act.sem_inc(s["sq2_done"], 1)
            for c in (1, 2, 3):
                act.sem_inc(s[f"sd{c}_done"], 1)
            run(act, ORDER["act"], one_step)

        @block.vector
        def _(dve):
            def gate(name, value):
                dve.wait_ge(s[name], value)
                dve.sem_inc(s["gate_dve"], 1)

            def by_head(ap, k):
                return ap[:, k, :].rearrange("p (h m d) -> p m h d", h=HEADS, m=KC)

            dve.wait_ge(s["idx_loaded"], 64)
            dve.tensor_copy(idx_f[0:CT, :, :], idx_raw[0:CT, :, :]).then_inc(s["idx_cast"], 1)
            turned = pF[1][0:ET, 0:3 * CT].rearrange("p (a t) -> p a t", a=3)
            dve.wait_ge(s["idx_turned"], 1)
            dve.tensor_copy(src_idx[:, :], turned[:, 0, :]).then_inc(s["idx_done"], 1)
            dve.tensor_copy(dst_idx[:, :], turned[:, 1, :]).then_inc(s["idx_done"], 1)
            dve.tensor_copy(col_f[0:ET, :], turned[:, 2, :]).then_inc(s["last_flag"], 1)
            dve.wait_ge(s["last_flag"], 1)
            dve.tensor_tensor(part_f[0:ET, :], turned[:, 1, :], col_f[0:ET, :], ALU.is_equal).then_inc(s["last_flag"], 1)
            dve.wait_ge(s["last_flag"], 2)
            dve.scalar_tensor_tensor(last_idx[:, :], part_f[0:ET, :], float(SKIP), turned[:, 1, :], ALU.mult, ALU.add)\
                .then_inc(s["idx_done"], 1)

            splits = [0]

            def split_lo(w, stage, permute):
                for k in range(KC):
                    splits[0] += 1
                    dve.wait_ge(s["split_hi"], splits[0])
                    if permute:
                        view = lambda t: t[:, k, :].rearrange("p (m h d) -> p m h d", m=KC, h=HEADS)
                        for m in range(KC):
                            ins = dve.tensor_tensor(view(w[1])[:, m], by_head(stage, k)[:, m], view(w[0])[:, m].bitcast(F32), ALU.subtract)
                    else:
                        ins = dve.tensor_tensor(w[1][:, k, :], stage[:, k, :], w[0][:, k, :].bitcast(F32), ALU.subtract)
                    ins.then_inc(s["split_lo"], 1)

            dve.wait_ge(s["w1_loaded"], 64)
            for k in range(KC):
                dve.tensor_scalar(w1[:, k, :], w1_raw[:, k, :], g1_col[:, k:k + 1], None, ALU.mult).then_inc(s["w1_done"], 1)
            split_lo(wq, w_stage["q"], True)
            dve.memset(hT[DFF:DFF + 1, :], 1.0).then_inc(s["ones_set"], 1)
            dve.wait_ge(s["w2_loaded"], 48)
            dve.tensor_tensor(w2[DFF:DFF + 1, :], w2[DFF:DFF + 1, :], be1_row, ALU.add).then_inc(s["w2_done"], 1)
            dve.wait_ge(s["b1_folded"], 1)
            dve.tensor_tensor(b1_col[:, :], pF[0][0:DFF, 0:1], b1_col[:, :], ALU.add).then_inc(s["b1_done"], 1)
            split_lo(wk, w_stage["k"], True)
            dve.wait_ge(s["iota_set"], 2)
            dve.tensor_copy(iota_n, iota_i).then_inc(s["iota_cast"], 1)
            dve.wait_ge(s["idx_done"], 3)
            dve.tensor_scalar(part_i[0:ET, :], dst_idx[:, :], 1, P - 1, ALU.logical_shift_right, ALU.bitwise_and).then_inc(s["digit_low"], 1)
            dve.tensor_scalar(col_i[0:ET, :], dst_idx[:, :], 8, 1, ALU.logical_shift_right, ALU.logical_shift_left).then_inc(s["digit_low"], 1)
            dve.tensor_scalar(low_i[0:ET, :], dst_idx[:, :], 1, None, ALU.bitwise_and).then_inc(s["digit_low"], 1)
            dve.wait_ge(s["digit_low"], 3)
            dve.tensor_copy(part_f[0:ET, :], part_i[0:ET, :]).then_inc(s["digit_done"], 1)
            dve.tensor_tensor(col_f[0:ET, :], col_i[0:ET, :], low_i[0:ET, :], ALU.add).then_inc(s["digit_done"], 1)
            dve.wait_ge(s["digit_done"], 2)
            dve.wait_ge(s["iota_cast"], 1)
            for c in range(CT // OHT):
                if c:
                    dve.wait_ge(s["counted"], c)
                for oh, digit, width in ((oh_p, part_f, P), (oh_c, col_f, CN)):
                    dve.tensor_tensor(oh, iota_n[0:ET, 0:width].rearrange("p (a n) -> p a n", a=1).broadcast_to([ET, OHT, width]),
                                      digit[0:ET, OHT * c:OHT * c + OHT].rearrange("p (t a) -> p t a", a=1).broadcast_to([ET, OHT, width]),
                                      ALU.is_equal).then_inc(s["onehot"], 1)
            dve.wait_ge(s["counted"], CT // OHT)
            dve.tensor_scalar(has_edge, pS[:, 0:CN], 0.5, float(SKIP), ALU.is_gt, ALU.mult).then_inc(s["flag_done"], 1)
            dve.wait_ge(s["flag_done"], 1)
            dve.tensor_tensor(node_idx[:, :], has_edge, node_i, ALU.add).then_inc(s["node_done"], 1)
            split_lo(wv, w_stage["v"], True)
            split_lo(wo, w_stage["o"], False)

            for name in ("n1_done", "t_done", "y_done", "z_rows", "rs1_done", "rs2_done", "rs3_done"):
                dve.sem_inc(s[name], 1)

            def one_step(i, step):
                if True:
                    if step == "TXD":
                        gate("row_loaded", 16 * (i + 1))
                        gate("alpha_done", i)
                        dve.tensor_tensor(nsame[:, :], dst_row[:, 1:EG + 1], dst_row[:, 0:EG], ALU.is_equal).then_inc(s["mask_eq"], 1)
                    elif step[:2] == "TX":
                        k, fill = int(step[3]), FILL[step]
                        if step[:3] == "TXD":
                            gate("xT_hi", 2 * KC * i + k + 1)
                            gate("pj_filled", 16 * i)
                        else:
                            gate("xT_hi", 2 * KC * i + KC + k + 1)
                            gate("pj_filled", 16 * i + 4)
                        dve.tensor_tensor(xT[1][:, k, :], pT[fill % 2][:, 0:EG], xT[0][:, k, :].bitcast(F32), ALU.subtract)\
                            .then_inc(s["xT_lo"], 1)
                    elif step[0] == "K":
                        m = int(step[1])
                        gate("pj_filled", 16 * i + 4 + m + 1)
                        gate("q_saved", 4 * i + m + 1)
                        if m == 0:
                            gate("score_done", i)
                        else:
                            gate("qk_acc", 3 * i + m - 1)
                        dve.tensor_tensor((qk if m == 0 else qk_m)[:, :], bank(step)[:, 0:EG], q[:, m, 0:EG], ALU.mult)\
                            .then_inc(s["qk_part"], 1)
                    elif step == "S":
                        gate("score_done", i + 1)
                        gate("mask_done", 2 * i + 2)
                        gate("max_carried", i)
                        dve.tensor_tensor_scan(mx[:, 1:EG + 1], far[:, :], pS[:, 0:EG], mx[:, 0:1], ALU.add, ALU.max)\
                            .then_inc(s["max_done"], 1)
                        gate("max_done", i + 1)
                        gate("alpha_done", i)
                        gate("scanned", 4 * i)
                        dve.tensor_tensor(ex[:, 1, :], pS[:, 0:EG], mx[:, 1:EG + 1], ALU.subtract).then_inc(s["weight_exp"], 1)
                        gate("exp_done", i + 1)
                        gate("z_carried", i)
                        gate("zT_done", i)
                        dve.tensor_tensor_scan(zs[:, 1:EG + 1], ex[:, 0, :], ex[:, 1, :], zs[:, 0:1], ALU.mult, ALU.add)\
                            .then_inc(s["z_done"], 1)
                        gate("z_done", i + 1)
                        dve.tensor_copy(zs[:, 0:1], zs[:, EG:EG + 1]).then_inc(s["z_carried"], 1)
                    elif step == "ZT":
                        gate("zT_done", i + 1)
                        dve.reciprocal(rz[:, :, :], pS[0:ET, :].rearrange("p (t h d) -> p t h d", t=4, h=HEADS)[:, :, :, 0])\
                            .then_inc(s["rz_done"], 1)
                        gate("rz_done", i + 1)
                        gate("rzb_done", i)
                        dve.tensor_copy(rz_all[:, :, :].rearrange("p t (h d) -> p (t h) d", h=HEADS),
                                        rz[:, :, :].rearrange("p t (h a) -> p (t h) a", a=1).broadcast_to([ET, 4 * HEADS, HD]))\
                            .then_inc(s["rz_spread"], 1)
                    elif step == "RZ":
                        gate("rzb_done", i + 1)
                        dve.tensor_tensor(ex[:, 1, :], pS[:, 0:EG], ex[:, 1, :], ALU.mult).then_inc(s["beta_done"], 1)
                        gate("beta_done", i + 1)
                        dve.scalar_tensor_tensor(ex[:, 0, :], ex[:, 1, :], 1.0, nsame[:, :], ALU.subtract, ALU.mult)\
                            .then_inc(s["alpha_done"], 1)
                    elif step[0] == "V":
                        weigh(i, int(step[1]), bank(step))
                    if "." not in step:
                        return
                    slot, what = step.split(".")
                    n = SLOTS.index(slot)
                    j = JOBS * i + n
                    edge = slot[0] == "E"
                    R = ET if edge else P

                    def inverse(c):
                        gate(f"sd{c}_done", j + 2)
                        gate({1: "n1_done", 2: "y_done", 3: "z_rows"}[c], j)
                        dve.reciprocal(rs[c - 1][n % 2][0:R, :], sd[c - 1][n % 2][0:R, :]).then_inc(s[f"rs{c}_done"], 1)
                        gate(f"rs{c}_done", j + 2)

                    if what == "sum1":
                        if edge:
                            gate("tr_filled", FILLS * i + END["C.T" if n == 4 else "D.T"])
                            gate("xr_done", j)
                            for t in range(2):
                                o = 2 * (n - 4) + t
                                gate("pj_filled", 16 * i + 12 + o + 1)
                                dve.tensor_tensor(n1[n % 2][0:R, t, :], bank(f"O{o}")[0:R, :], xd[:, o, :], ALU.add)\
                                    .then_inc(s["hx_done"], 1)
                            gate("hx_done", 4 * i + 2 * (n - 4) + 2)
                        else:
                            gate(f"xin_loaded{n % 2}", 16 * (2 * i + n // 2 + 1))
                        source = n1[n % 2] if edge else xin[n % 2]
                        gate("mv1_done", 2 * j)
                        for t in range(2):
                            dve.bn_stats(st[0:R, t, :], source[0:R, t, :]).then_inc(s["st1_done"], 1)
                        gate("n1_done", j)
                        gate("sd1_done", j)
                        for t in range(2):
                            gate("st1_done", 2 * j + t + 1)
                            dve.bn_aggr(mv[n % 2][0:R, t, :], st[0:R, t, :]).then_inc(s["mv1_done"], 1)
                    elif what == "norm1":
                        inverse(1)
                        if not edge:
                            gate("h_filled", j)
                            gate("xr_done", j)
                        source = n1[n % 2] if edge else xin[n % 2]
                        for t in range(2):
                            ins = dve.tensor_scalar(n1[n % 2][0:R, t, :], source[0:R, t, :], mv[n % 2][0:R, t, 0:1], rs[0][n % 2][0:R, t:t + 1],
                                                    ALU.subtract, ALU.mult)
                        ins.then_inc(s["n1_done"], 1)
                    elif what == "x2":
                        gate("xr_done", j + 2)
                        gate("nm2_done", j)
                        for t in range(2):
                            gate("f_filled", 2 * j + t + 1)
                            dve.scalar_tensor_tensor(x2[n % 2][0:R, t, :], pF[(t + 1) % 2][0:R, :], 1.0, x2[n % 2][0:R, t, :],
                                                     ALU.mult, ALU.add, accum_out=sums[1][0:R, t:t + 1]).then_inc(s["x2_done"], 1)
                        gate("x2_done", 2 * j + 2)
                        gate("t_done", j)
                        gate("sq2_done", j)
                        dve.tensor_scalar(nmean[1][n % 2][0:R, :], sums[1][0:R, :], -1.0 / D, None, ALU.mult).then_inc(s["nm2_done"], 1)
                    elif what == "t":
                        gate("nm2_done", j + 1)
                        gate(f"out_{SLOTS[n - 2]}", 32 * (i + (n >= 2)))
                        for t in range(2):
                            ins = dve.scalar_tensor_tensor(y[n % 2][0:R, t, :], x2[n % 2][0:R, t, :], nmean[1][n % 2][0:R, t:t + 1], g2_all[0:R, :],
                                                           ALU.add, ALU.mult)
                        ins.then_inc(s["t_done"], 1)
                    elif what == "norm2":
                        gate("t_done", j + 2)
                        inverse(2)
                        gate("xb_done", j + 1)
                        gate("nm3_done", j)
                        for t in range(2):
                            ins = dve.scalar_tensor_tensor(y[n % 2][0:R, t, :], y[n % 2][0:R, t, :], rs[1][n % 2][0:R, t:t + 1], xb[n % 2][0:R, t, :],
                                                           ALU.mult, ALU.add, accum_out=sums[2][0:R, t:t + 1])
                        ins.then_inc(s["y_done"], 1)
                        gate("y_done", j + 2)
                        gate("z_rows", j)
                        dve.tensor_scalar(nmean[2][n % 2][0:R, :], sums[2][0:R, :], -1.0 / D, None, ALU.mult).then_inc(s["nm3_done"], 1)
                    elif what == "norm3":
                        inverse(3)
                        for t in range(2):
                            ins = dve.tensor_scalar(y[n % 2][0:R, t, :], y[n % 2][0:R, t, :], nmean[2][n % 2][0:R, t:t + 1], rs[2][n % 2][0:R, t:t + 1],
                                                    ALU.add, ALU.mult)
                        ins.then_inc(s["z_rows"], 1)

            def weigh(i, m, v):
                gate("pj_filled", 16 * i + 8 + m + 1)
                gate("beta_done", i + 1)
                gate("scanned", 4 * i + max(m - 1, 0))
                dve.tensor_tensor(wgt[:, m % 2, :], v[:, 0:EG], ex[:, 1, :], ALU.mult).then_inc(s["weighted"], 1)
                gate("weighted", 4 * i + m + 1)
                gate("alpha_done", i + 1)
                gate("a_lo", 4 * i + max(m - 1, 0))
                gate("carried", 4 * i)
                dve.tensor_tensor_scan(att[:, m % 2, :], ex[:, 0, :], wgt[:, m % 2, :], carry[:, m:m + 1], ALU.mult, ALU.add)\
                    .then_inc(s["scanned"], 1)
                gate("scanned", 4 * i + m + 1)
                dve.tensor_copy(carry[:, m:m + 1], att[:, m % 2, EG - 1:EG]).then_inc(s["carried"], 1)
                gate("a_hi", 4 * i + m + 1)
                gate("pj_filled", 16 * i)
                dve.tensor_tensor(aT[1][:, m, :], att[:, m % 2, :], aT[0][:, m, :].bitcast(F32), ALU.subtract)\
                    .then_inc(s["a_lo"], 1)

            run(dve, ORDER["dve"], one_step)

        @block.tensor
        def _(pe):
            pe.wait_ge(s["ident_done"], 1)
            pe.wait_ge(s["idx_cast"], 1)
            turned = pF[1][0:ET, 0:3 * CT].rearrange("p (a t) -> p a t", a=3)
            for a in range(3):
                ins = pe.transpose(turned[:, a, :], idx_f[0:CT, a, :], ident[0:CT, 0:CT])
            ins.then_inc(s["idx_turned"], 1)
            pe.wait_ge(s["w1_loaded"], 64)
            for k in range(KC):
                ins = pe.matmul(pF[0][0:DFF, 0:1], w1_raw[:, k, :], be1_col[:, k:k + 1], start=(k == 0), stop=(k == KC - 1))
            ins.then_inc(s["b1_folded"], 1)
            for c in range(CT // OHT):
                pe.wait_ge(s["onehot"], 2 * c + 2)
                for t in range(OHT):
                    ins = pe.matmul(pS[:, 0:CN], oh_p[:, t, :], oh_c[:, t, :], start=(c + t == 0), stop=(c == CT // OHT - 1 and t == OHT - 1))
                ins.then_inc(s["counted"], 1)
            pe.wait_ge(s["head_done"], 1)
            pe.wait_ge(s["ones_set"], 1)
            pe.wait_ge(s["b1_done"], 1)
            pe.wait_ge(s["w1_done"], KC)
            pe.wait_ge(s["w2_done"], 1)
            pe.wait_ge(s["node_done"], 1)
            pe.wait_ge(s["split_lo"], 4 * KC)

            def split_product(acc, left, right, n):
                for k in range(n):
                    for a, b in ((0, 0), (0, 1), (1, 0)):
                        ins = pe.matmul(acc, left(a, k), right(b, k), start=(k == 0 and a == b), stop=(k == n - 1 and a == 1))
                return ins

            def one_step(i, step):
                def bank_free(fill):
                    kind, count = READER[fill]
                    pe.wait_ge(s[kind], (2 * KC if kind == "xT_lo" else 2 * JOBS) * i + count)

                if True:
                    if step[:2] == "TX":
                        rows_in = xd if step[:3] == "TXD" else xs
                        k, fill = int(step[3]), FILL[step]
                        if k == 0:
                            pe.wait_ge(s["xd_loaded" if step[:3] == "TXD" else "xs_loaded"], 64 * (i + 1))
                        bank_free(fill)
                        for t in range(4):
                            ins = pe.transpose(pT[fill % 2][:, ET * t:ET * t + ET], rows_in[:, t, P * k:P * k + P], ident[0:ET, 0:ET])
                        ins.then_inc(s["tr_filled"], 1)
                    elif "." not in step and step[0] in "QKV":
                        m = int(step[1])
                        w = {"Q": wq, "K": wk, "V": wv}[step[0]]
                        pe.wait_ge(s["xT_lo"], 2 * KC * i + (KC if step[0] == "Q" else 2 * KC))
                        free_bank(i, PLACE[step])
                        split_product(bank(step)[:, 0:EG], lambda a, k: w[a][:, k, P * m:P * m + P], lambda b, k: xT[b][:, k, :], KC)\
                            .then_inc(s["pj_filled"], 1)
                    elif step == "S":
                        pe.wait_ge(s["qk_acc"], 3 * i + 3)
                        pe.wait_ge(s["beta_done"], i)
                        pe.matmul(pS[:, 0:EG], same_head[:, :], qk[:, :], start=True, stop=True).then_inc(s["score_done"], 1)
                    elif step == "ZT":
                        pe.wait_ge(s["z_done"], i + 1)
                        pe.wait_ge(s["weight_exp"], i + 1)
                        for t in range(4):
                            ins = pe.transpose(pS[0:ET, P * t:P * t + P], zs[:, 1 + ET * t:1 + ET * t + ET], ident[:, :])
                        ins.then_inc(s["zT_done"], 1)
                    elif step == "RZ":
                        pe.wait_ge(s["rz_spread"], i + 1)
                        for t in range(4):
                            ins = pe.transpose(pS[:, ET * t:ET * t + ET], rz_all[:, t, :], ident[0:ET, 0:ET])
                        ins.then_inc(s["rzb_done"], 1)
                    elif "." not in step and step[0] == "O":
                        t = int(step[1])
                        pe.wait_ge(s["a_lo"], 4 * i + 4)
                        free_bank(i, PLACE[step])
                        split_product(bank(step)[0:ET, :], lambda a, m: aT[a][:, m, ET * t:ET * t + ET], lambda b, m: wo[b][:, m, :], KC)\
                            .then_inc(s["pj_filled"], 1)
                    if "." not in step:
                        return
                    slot, what = step.split(".")
                    n = SLOTS.index(slot)
                    j = JOBS * i + n
                    edge = slot[0] == "E"
                    R = ET if edge else P
                    if what == "T":
                        pe.wait_ge(s["n1_done"], j + 2)
                        for half in range(2):
                            fill = FILL[step] + half
                            bank_free(fill)
                            for c in range(2):
                                k = 2 * half + c
                                for t in range(2):
                                    ins = pe.transpose(pT[fill % 2][:, NB * c + R * t:NB * c + R * t + R], n1[n % 2][0:R, t, P * k:P * k + P], ident[0:R, 0:R])
                            ins.then_inc(s["tr_filled"], 1)
                    elif what == "F1":
                        pe.wait_ge(s["nT_done"], 2 * j + 2)
                        pe.wait_ge(s["x2_done"], 2 * j)
                        for k in range(KC):
                            ins = pe.matmul(pF[0][0:DFF, 0:2 * R], w1[:, k, :], nT[:, k, 0:2 * R], start=(k == 0), stop=(k == KC - 1))
                        ins.then_inc(s["h_filled"], 1)
                    elif what == "F2":
                        pe.wait_ge(s["h_done"], j + 1)
                        for t in range(2):
                            pe.matmul(pF[(t + 1) % 2][0:R, :], hT[:, R * t:R * t + R], w2[:, :], start=True, stop=True)\
                                .then_inc(s["f_filled"], 1)

            kinds, counts = [], {"xT_lo": 0, "nT_done": 0}
            for step in pe_steps:
                for _ in range(END[step] - FILL[step] if step in FILL else 0):
                    kinds.append("xT_lo" if step[0] == "T" else "nT_done")
            assert kinds[-2:] == ["nT_done"] * 2
            READER = [("nT_done", 0)] * 2
            for kind in kinds[:-2]:
                counts[kind] += 1
                READER.append((kind, counts[kind]))

            def free_bank(i, place):
                before = [n for n in range(place) if BANK[n] == BANK[place]]
                if before:
                    kind, m = divmod(before[-1], 4)
                    pe.wait_ge(s[("q_saved", "qk_part", "weighted", "hx_done")[kind]], 4 * i + m + 1)
                else:
                    pe.wait_ge(s["hx_done"], 4 * i)

            pe.sem_inc(s["h_filled"], 1)
            run(pe, ORDER["pe"], one_step)


_INS = ["x", "src", "dst", "L0_gnn_Wq", "L0_gnn_Wk", "L0_gnn_Wv", "L0_gnn_Wo", "L0_gnn_ln1_g", "L0_gnn_ln1_b",
        "L0_gnn_ln2_g", "L0_gnn_ln2_b", "L0_gnn_W1", "L0_gnn_b1", "L0_gnn_W2", "L0_gnn_b2"]


def kernel(**inputs):
    import numpy as _np
    import concourse.bacc as _bacc
    from concourse import mybir as _mybir
    from concourse.bass_utils import run_bass_kernel_spmd as _run

    nc = _bacc.Bacc("TRN2", target_bir_lowering=False, num_devices=1)
    arrays, args = {}, []
    for name in _INS:
        a = _np.ascontiguousarray(inputs[name])
        arrays[f"in_{name}_dram"] = a
        args.append(nc.dram_tensor(f"in_{name}_dram", a.shape, _mybir.dt.from_np(a.dtype), kind="ExternalInput").ap())
    out = nc.dram_tensor("out_0_dram", inputs["x"].shape, _mybir.dt.float32, kind="ExternalOutput").ap()
    graph_attention(nc, *args, out)
    r = _run(nc, [arrays], core_ids=[0])
    return r.results[0]["out_0_dram"]
```

```python
from contextlib import ExitStack

import concourse.bass as bass
from concourse import mybir

F32 = mybir.dt.float32
F32R = mybir.dt.float32r
BF16 = mybir.dt.bfloat16
I32 = mybir.dt.int32
U32 = mybir.dt.uint32
ALU = mybir.AluOpType
ACT = mybir.ActivationFunctionType

HEADS = 8
EPS = 1e-5
SKIP = 1 << 20
FAR = 3.0e38

ORDER = {
    "pe": """
A.T- Q0- Q1- A.F1- Q2- Q3- TXS0- TXS1- A.F2- TXS2- TXS3- B.T- K0- K1- B.F1- K2- C.T- B.F2- K3- C.F1-
D.T- S- C.F2- V0- ZT- D.F1- RZ- V1- V2- V3- D.F2- O0- O1- O2- O3- E0.T- E0.F1- E1.T- E0.F2- TXD0
TXD1 E1.F1- TXD2 TXD3 E1.F2-
""".split(),
    "act": """
B.T- Q2- Q3- A.sq- CP1- D.sd- CP0- B.F1- A.sq3- C.T- B.sq- A.z- D.T- C.F1- B.sq3- S- V0- C.sq- B.z-
V1- V2- D.F1- V3- C.sq3- E0.sd- D.sq- E0.T- E1.sd- E0.F1- C.z- D.sq3- E1.T- A.sd TXD0 B.sd TXD1
E0.sq- E1.F1- TXD2 TXD3 D.z- E0.sq3- A.T Q0 E1.sq- A.F1 E0.z- E1.sq3- TXS0 C.sd TXS1 TXS2 TXS3 Q1
E1.z-
""".split(),
    "dve": """
D.norm1- K1- A.y- A.m3- K2- B.x2- B.m2- B.t- K3- A.r3- A.shift- B.r2- B.y- B.m3- S- EX- C.x2- Z-
B.r3- ZT- C.m2- C.t- RZ- W0- ZC- N0- G0- B.shift- W1- MC- W2- N1- L0- N2- W3- G1- G2- L1- N3- L2-
L3- D.x2- C.r2- D.m2- C.y- C.m3- D.t- H0- H1- E0.sum1- C.r3- E0.mv- E0.r1- C.shift- E0.norm1- H2-
H3- D.r2- E1.sum1- E1.mv- E1.r1- E1.norm1- D.y- A.sum1 A.mv D.m3- E0.x2- G3- B.sum1 E0.m2- B.mv
D.r3- A.r1 TXD0 E0.t- TXD1 A.norm1 TXD2 TXD3 D.shift- E0.r2- E0.y- E0.m3- E1.x2- B.r1 E1.m2- E0.r3-
E1.t- E1.r2- B.norm1 E0.shift- E1.y- E1.m3- C.sum1 E1.r3- C.mv E1.shift- TXS0 TXD C.r1 TXS1 TXS2
TXS3 D.sum1 A.x2 A.m2 C.norm1 A.t K0 D.mv A.r2 D.r1
""".split(),
    "pool": """
GXS- B.out- D.xr- E0.xb- E0.xr- GXD- C.out- E1.xb- E1.xr- D.out- A.xb S A.xr IE- B.xb TXD E0.out-
E1.out- B.xr C.xr K1 K2 IN C.xb K3 A.out D.xb
""".split(),
}
SLOTS = ["A", "B", "C", "D", "E0", "E1"]
JOBS = len(SLOTS)
FILLS = 4 + 4 + 2 * JOBS


class Count:

    def __init__(self, register, rate=1, ahead=0):
        self.register, self.rate, self.ahead = register, rate, ahead

    def __add__(self, n):
        return Count(self.register, self.rate, self.ahead + n)

    def __sub__(self, n):
        return self + -n

    def __mul__(self, n):
        return Count(self.register, self.rate * n, self.ahead * n)

    __radd__, __rmul__ = __add__, __mul__

    def is_round(self, n):
        return isinstance(self.register, int) and self.rate * self.register + self.ahead == n

    def value(self):
        if self.rate == 0:
            return self.ahead
        return self.rate * self.register + self.ahead


class Waits:

    def __init__(self, wait):
        self.wait, self.seen = wait, {}

    def begin_round(self):
        self.seen = {}

    def __call__(self, name, count):
        if isinstance(count.register, int) and count.value() <= 0:
            return
        if name in self.seen and self.seen[name] >= count.ahead:
            return
        self.seen[name] = count.ahead
        self.wait(name, count.value())


def graph_attention(nc, x, src, dst, Wq, Wk, Wv, Wo, g1, be1, g2, be2, W1, b1, W2, b2, out):
    N, D = x.shape
    E = src.shape[0]
    DFF = W1.shape[1]
    P = 128
    KC = D // P
    HD = P // HEADS
    DK = D // HEADS
    ET = 125
    EG = KC * ET
    ROUNDS = E // EG
    NB = 2 * P
    TAIL = (N - (4 * ROUNDS - 1) * NB) // 2
    CT = E // ET
    CN = 8 * ROUNDS
    assert E == ROUNDS * EG and N <= 4 * ROUNDS * NB and TAIL > 0 and D == 512 and 2 * DFF == P

    ctx = ExitStack()
    with ctx:
        def sb(name, shape, dt=F32):
            return ctx.enter_context(nc.sbuf_tensor(name, shape, dt))

        def sem(name):
            return ctx.enter_context(nc.semaphore(name))

        ident = sb("ident", [P, P])
        same_head = sb("same_head", [P, P])
        wq = [sb(f"wq_{n}", [P, KC, D], F32R) for n in ("hi", "lo")]
        wk = [sb(f"wk_{n}", [P, KC, D], F32R) for n in ("hi", "lo")]
        wv = [sb(f"wv_{n}", [P, KC, D], F32R) for n in ("hi", "lo")]
        wo = [sb(f"wo_{n}", [P, KC, D], F32R) for n in ("hi", "lo")]
        w1 = sb("w1", [P, KC, DFF])
        w2 = sb("w2", [DFF + 1, D])
        g1_all = sb("g1_all", [P, D])
        g2_all = sb("g2_all", [P, D])
        be2_all = sb("be2_all", [P, D])
        g1_col = sb("g1_col", [P, KC])
        be1_col = sb("be1_col", [P, KC])
        b1_col = sb("b1_col", [DFF, 1])
        eps_col = sb("eps_col", [P, 1])
        src_idx = sb("src_idx", [ET, CT], I32)
        dst_idx = sb("dst_idx", [ET, CT], I32)
        last_idx = sb("last_idx", [ET, CT], I32)
        node_idx = sb("node_idx", [P, CN], I32)
        src_now = sb("src_now", [ET, 4], I32)
        dst_now = sb("dst_now", [ET, 4], I32)
        last_now = sb("last_now", [ET, 4], I32)
        node_now = sb("node_now", [P, 8], I32)
        xs = sb("xs", [ET, 4, D])
        xd = sb("xd", [ET, 4, D])
        xe = sb("xe", [ET, 4, D])
        aT = [sb(f"aT_{n}", [P, KC, EG], F32R) for n in ("hi", "lo")]
        q = sb("q", [P, KC, D])
        xT = [sb(f"xT_{n}", [P, KC, EG], F32R) for n in ("hi", "lo")]
        qk = sb("qk", [P, EG])
        qk_m = sb("qk_m", [P, EG])
        dst_row = sb("dst_row", [P, EG + 1], I32)
        far = sb("far", [P, EG])
        nsame = sb("nsame", [P, EG])
        mx = sb("mx", [P, EG + 1])
        zs = sb("zs", [P, EG + 1])
        ex = sb("ex", [P, 2, EG])
        rz = sb("rz", [ET, 4, HEADS])
        rz_all = q[0:ET, 3, :].rearrange("p (t n) -> p t n", t=4)
        wgt = q[:, 0:2, 0:EG]
        att = q[:, 2:4, 0:EG]
        carry = sb("carry", [P, KC])
        xin = [sb(f"xin{n}", [P, 2, D]) for n in range(2)]
        xb = [sb(f"xb{n}", [P, 2, D]) for n in range(2)]
        rows = sb("rows", [P, 12, D])
        n1 = [rows[:, 2 * n:2 * n + 2, :] for n in (0, 2)]
        x2 = [rows[:, 2 * n:2 * n + 2, :] for n in (1, 3)]
        y = [rows[:, 2 * n:2 * n + 2, :] for n in (4, 5)]
        squares = [None] + [sb(f"squares{n}", [P, 2, D], BF16) for n in (2, 3)]
        nT = sb("nT", [P, KC, NB])
        hT = sb("hT", [DFF + 1, NB])
        st = sb("st", [P, 2, 6])
        mv = [sb(f"mv{n}", [P, 2, 2]) for n in range(2)]
        sums = [None] + [sb(f"sums{n}", [P, 2]) for n in (2, 3)]
        sq = [None] + [sb(f"sq{n}", [P, 2]) for n in (2, 3)]
        nmean = [None] + [[sb(f"nmean{c}_{n}", [P, 2]) for n in range(2)] for c in (2, 3)]
        sd = [[sb(f"sd{c}_{n}", [P, 2]) for n in range(2)] for c in (1, 2, 3)]
        shift = [None, None, [sb(f"shift3_{n}", [P, 2]) for n in range(2)]]
        rs = [[sb(f"rs{c}_{n}", [P, 2]) for n in range(2)] for c in (1, 2, 3)]

        pT = [ctx.enter_context(nc.psum_tensor(f"pT{n}", [P, 512], F32)) for n in range(2)]
        pP = [ctx.enter_context(nc.psum_tensor(f"pP{n}", [P, 512], F32)) for n in range(3)]
        pS = ctx.enter_context(nc.psum_tensor("pS", [P, 512], F32))
        pF = [ctx.enter_context(nc.psum_tensor(f"pF{n}", [P, 512], F32)) for n in range(2)]

        w_stage = {"q": q[:, :, :], "k": rows[:, 0:4, :], "v": rows[:, 4:8, :], "o": rows[:, 8:12, :]}
        w1_raw = xin[0][:, 0, 0:KC * DFF].rearrange("p (k f) -> p k f", k=KC)
        be1_row = xb[1][DFF:DFF + 1, 0, :]
        idx_raw = ex[:, :, :].rearrange("p a b -> p (a b)")[:, 0:3 * ET].bitcast(I32).rearrange("p (a b) -> p a b", a=3)
        idx_f = ex[:, :, :].rearrange("p a b -> p (a b)")[:, 512:512 + 3 * ET].rearrange("p (a b) -> p a b", a=3)
        OHT = 8
        onehots = [[xe[:, 2 * n:2 * n + 2, :].rearrange("p a b -> p (a b)").bitcast(BF16)[:, batch * OHT * P:batch * OHT * P + OHT * width]
                    .rearrange("p (t n) -> p t n", t=OHT) for n, width in enumerate((P, CN))] for batch in range(2)]
        part_b, col_b, iota_b = (nsame[:, :].bitcast(BF16)[:, P * n:P * n + width] for n, width in enumerate((CT, CT, P)))
        iota_i = qk_m[:, 0:P].bitcast(I32)
        node_i = qk_m[:, P:P + CN].bitcast(I32)
        part_i = qk[:, P:P + CT].bitcast(I32)
        col_i = qk[:, 2 * P:2 * P + CT].bitcast(I32)
        low_i = qk[:, 3 * P:3 * P + CT].bitcast(I32)
        part_f = qk_m[:, 2 * P:2 * P + CT]
        col_f = qk_m[:, 2 * P + CT:2 * P + 2 * CT]
        has_edge = qk_m[:, 3 * P:3 * P + CN]

        names = """idx_loaded wq_loaded wk_loaded wv_loaded wo_loaded w1_loaded w2_loaded all_loaded
        row_loaded ident_set ident_done head_set head_done zero_set idx_cast idx_turned idx_done last_flag
        split_hi split_lo split_lo_pool w1_done w2_done b1_folded b1_done ones_set
        iota_set iota_cast digit_low digit_done onehot counted flag_done node_done init_done
        gate_sp gate_pool gate_act gate_dve
        src_picked dst_picked last_picked node_picked xs_loaded xd_loaded xin_loaded0 xin_loaded1
        mask_eq mask_done xe_done
        tr_filled xT_hi xT_lo nT_done pj_filled q_saved qk_part qk_acc score_done max_done max_carried
        decay_half decay_done weight_exp exp_done z_done z_carried zT_done rz_done rz_spread rzb_done beta_done alpha_done
        weighted scanned carried a_hi a_lo
        hx_done st1_done mv1_done sd1_done rs1_done n1_done xb_done xr_done
        h_filled h_done f_filled x2_done nm2_done sq2_done sd2_done rs2_done t_done
        y_done nm3_done sq3_done sd3_done rs3_done shift3_done z_rows out_A out_B out_C out_D out_E0 out_E1""".split()
        s = {name: sem(name) for name in names}

        FILL, END, fills = {}, {}, 0
        pe_steps = [step for step in ORDER["pe"] if not step.endswith("-")] + [step[:-1] for step in ORDER["pe"] if step.endswith("-")]
        for step in pe_steps:
            if step[:2] == "TX" or step.endswith(".T"):
                FILL[step] = fills
                fills += 2 if step.endswith(".T") else 1
                END[step] = fills
        PLACE = {f"{kind}{m}": 4 * n + m for n, kind in enumerate("QKVO") for m in range(4)}
        BANK = [n % 3 for n in range(15)] + [1]

        def bank(step):
            return pP[BANK[PLACE[step]]]


        def run(engine, gate, order, one_step, last_differs=False):
            late = [step for step in order if step.endswith("-")]

            def one_round(i):
                gate.begin_round()
                for step in order:
                    if not step.endswith("-"):
                        one_step(Count(i), step)
                    elif not isinstance(i, int) or i > 0:
                        one_step(Count(i) - 1, step[:-1])

            one_round(0)
            one_round(1)
            with engine.Fori(2, ROUNDS - 1 if last_differs else ROUNDS) as i:
                one_round(i)
            gate.begin_round()
            if last_differs:
                one_round(ROUNDS - 1)
            for step in late:
                one_step(Count(ROUNDS - 1), step[:-1])

        block = ctx.enter_context(nc.Block())

        def bcast_rows(ap, n):
            return bass.AP(tensor=ap.tensor, offset=ap.offset, ap=[[0, P], [1, n]])

        @block.sync
        def _(sp):
            def gate(name, value):
                if isinstance(value, int) and value <= 0:
                    return
                sp.wait_ge(s[name], value)
                sp.sem_inc(s["gate_sp"], 1)

            def rows_of(block_no, parts=P):
                return x[bass.ds(NB * block_no, 2 * parts), :].rearrange("(p t) d -> p t d", t=2)

            def load_dst_row(i):
                sp.dma_start(dst_row[:, :], bass.AP(tensor=dst.tensor, offset=dst.offset + (EG * i - 1), ap=[[0, P], [1, EG + 1]]))\
                    .then_inc(s["row_loaded"], 16)

            sp.dma_start(idx_raw[0:CT, 0, :], src.rearrange("(t e) -> t e", e=ET)).then_inc(s["idx_loaded"], 16)
            sp.dma_start(idx_raw[0:CT, 1, :], dst.rearrange("(t e) -> t e", e=ET)).then_inc(s["idx_loaded"], 16)
            sp.wait_ge(s["zero_set"], 2)
            sp.dma_start(idx_raw[0:CT - 1, 2, :], dst[1:1 + (CT - 1) * ET].rearrange("(t e) -> t e", e=ET))\
                .then_inc(s["idx_loaded"], 16)
            sp.dma_start(idx_raw[CT - 1:CT, 2, 0:ET - 1], dst[1 + (CT - 1) * ET:E].rearrange("(t e) -> t e", t=1))\
                .then_inc(s["idx_loaded"], 16)
            sp.dma_start(w_stage["q"], Wq.rearrange("(k p) n -> p k n", p=P)).then_inc(s["wq_loaded"], 16)
            with nc.allow_non_contiguous_dma("short columns, once"):
                sp.dma_start(g1_col[:, :], g1.rearrange("(k p) -> p k", p=P)).then_inc(s["w1_loaded"], 16)
                sp.dma_start(be1_col[:, :], be1.rearrange("(k p) -> p k", p=P)).then_inc(s["w1_loaded"], 16)
                sp.dma_start(b1_col[:, :], b1.rearrange("(f a) -> f a", a=1)).then_inc(s["w1_loaded"], 16)
            sp.dma_start(w1_raw, W1.rearrange("(k p) f -> p k f", p=P)).then_inc(s["w1_loaded"], 16)
            sp.dma_start(w2[0:DFF, :], W2).then_inc(s["w2_loaded"], 16)
            sp.dma_start(w2[DFF:DFF + 1, :], b2.rearrange("(a n) -> a n", a=1)).then_inc(s["w2_loaded"], 16)
            sp.dma_start(be1_row, be1.rearrange("(a n) -> a n", a=1)).then_inc(s["w2_loaded"], 16)
            sp.dma_start(dst_row[:, 1:EG + 1], bcast_rows(dst, EG)).then_inc(s["row_loaded"], 16)
            sp.dma_start(w_stage["k"], Wk.rearrange("(k p) n -> p k n", p=P)).then_inc(s["wk_loaded"], 16)
            sp.dma_start(w_stage["v"], Wv.rearrange("(k p) n -> p k n", p=P)).then_inc(s["wv_loaded"], 16)
            for tile, vec in ((g1_all, g1), (be2_all, be2), (g2_all, g2)):
                sp.dma_start(tile[:, :], bcast_rows(vec, D)).then_inc(s["all_loaded"], 16)
            wo_rows = Wo.rearrange("(h m d) n -> h d m n", h=HEADS, m=KC)
            for h in range(HEADS):
                sp.dma_start(w_stage["o"][HD * h:HD * h + HD, :, :], wo_rows[h]).then_inc(s["wo_loaded"], 16)
            sp.wait_ge(s["b1_folded"], 1)
            sp.wait_ge(s["w1_done"], KC)
            for n in range(2):
                sp.dma_start(xin[n][:, :, :], rows_of(n)).then_inc(s[f"xin_loaded{n}"], 16)

            def round_loads(i, last):
                def load(n, block_no, parts=P):
                    gate("n1_done", JOBS * i + n + 2)
                    gate("xb_done", JOBS * i + n + 1)
                    sp.dma_start(xin[n % 2][0:parts, :, :], rows_of(block_no, parts)).then_inc(s[f"xin_loaded{n % 2}"], 16)

                load(0, 4 * i + 2)
                load(1, 4 * i + 3, TAIL if last else P)
                if last:
                    return
                gate("mask_eq", i + 1)
                load_dst_row(i + 1)
                load(2, 4 * i + 4)
                load(3, 4 * i + 5)

            round_loads(0, last=False)
            with sp.Fori(1, ROUNDS - 1) as i:
                round_loads(i, last=False)
            round_loads(ROUNDS - 1, last=True)

        @block.gpsimd
        def _(pool):
            def wait(name, value):
                pool.wait_ge(s[name], value)
                pool.sem_inc(s["gate_pool"], 1)

            gate = Waits(wait)

            pool.memset(idx_raw[0:64, 2, :], -1).then_inc(s["zero_set"], 1)
            pool.memset(dst_row[:, 0:1], -1).then_inc(s["zero_set"], 1)
            pool.memset(ident[:, :], 0.0).then_inc(s["ident_set"], 1)
            pool.memset(same_head[:, :], DK ** -0.5).then_inc(s["head_set"], 1)
            pool.wait_ge(s["ident_set"], 1)
            pool.affine_select(out=ident[:, :], in_=ident[:, :], compare_op=ALU.not_equal, fill=1.0, base=0,
                               pattern=[[-1, P]], channel_multiplier=1).then_inc(s["ident_done"], 1)
            heads = same_head[:, :].rearrange("p (h d) -> p h d", h=HEADS)
            pool.wait_ge(s["head_set"], 1)
            pool.affine_select(out=heads, in_=heads, compare_op=ALU.is_ge, fill=0.0, base=0,
                               pattern=[[-HD, HEADS], [0, HD]], channel_multiplier=1).then_inc(s["head_set"], 1)
            pool.wait_ge(s["head_set"], 2)
            pool.affine_select(out=heads, in_=heads, compare_op=ALU.is_ge, fill=0.0, base=HD - 1,
                               pattern=[[HD, HEADS], [0, HD]], channel_multiplier=-1).then_inc(s["head_done"], 1)
            pool.iota(iota_i, pattern=[[1, P]], base=0, channel_multiplier=0).then_inc(s["iota_set"], 1)
            pool.iota(node_i.rearrange("p (b t) -> p b t", t=2), pattern=[[NB, CN // 2], [1, 2]], base=0,
                      channel_multiplier=2).then_inc(s["iota_set"], 1)
            pool.memset(eps_col[:, :], EPS).then_inc(s["init_done"], 1)
            pool.memset(mx[:, 0:1], 0.0).then_inc(s["init_done"], 1)
            pool.memset(zs[:, 0:1], 0.0).then_inc(s["init_done"], 1)
            pool.memset(carry[:, :], 0.0).then_inc(s["init_done"], 1)

            def pick(now, table, name, i, width, *free):
                for last_use in free:
                    gate(*last_use)
                pool.tensor_copy(now[:, :], table[:, bass.ds((i * width).value(), width)]).then_inc(s[name], 1)

            def gather(dest, index, name):
                pool.indirect_dma_start(dest, None, x, bass.IndirectOffsetOnAxis(ap=index.bitcast(U32), axis=0),
                                        bounds_check=N - 1, oob_is_err=False).then_inc(s[name], 16)

            def scatter(rows_ap, index, name):
                pool.indirect_dma_start(out, bass.IndirectOffsetOnAxis(ap=index.bitcast(U32), axis=0), rows_ap, None,
                                        bounds_check=N - 1, oob_is_err=False).then_inc(s[name], 16)

            def gather_group(which, i, first):
                now, table, rows_in, end = {"dst": (dst_now, dst_idx, xd, END["TXD3"]), "src": (src_now, src_idx, xs, END["TXS3"])}[which]
                loaded = "xd_loaded" if which == "dst" else "xs_loaded"
                pick(now, table, f"{which}_picked", i, 4, *([] if first else [(loaded, 64 * i)]))
                gate(f"{which}_picked", i + 1)
                if not first:
                    gate("tr_filled", FILLS * (i - 1) + end)
                    if which == "dst":
                        gate("xe_done", 2 * i)
                for t in range(4):
                    gather(rows_in[:, t, :], now[:, t:t + 1], loaded)

            pool.wait_ge(s["idx_done"], 3)
            gather_group("dst", Count(0), first=True)
            gather_group("src", Count(0), first=True)

            def one_step(i, step):
                last = i.is_round(ROUNDS - 1)
                def masks():
                    gate("mask_eq", i + 1)
                    gate("decay_done", i)
                    pool.tensor_scalar(far[:, :], nsame[:, :], FAR, -FAR, ALU.mult, ALU.add).then_inc(s["mask_done"], 1)
                    gate("mask_done", 2 * i + 1)
                    pool.tensor_scalar(nsame[:, :], nsame[:, :], -1.0, 0.0, ALU.mult, ALU.add).then_inc(s["mask_done"], 1)

                if step == "TXD":
                    masks()
                elif step == "IE":
                    pick(last_now, last_idx, "last_picked", i, 4, ("out_E0", 32 * i), ("out_E1", 32 * i))
                elif step == "IN":
                    gate("node_done", 0 * i + 1)
                    pick(node_now, node_idx, "node_picked", i, 8, *[(f"out_{block_slot}", 32 * i) for block_slot in "ABCD"])
                elif step[0] == "K" and step != "K0":
                    m = int(step[1])
                    gate("qk_part", 4 * i + m + 1)
                    if m > 1:
                        gate("qk_acc", 3 * i + m - 1)
                    pool.tensor_tensor(qk[:, :], qk[:, :], qk_m[:, :], ALU.add).then_inc(s["qk_acc"], 1)
                elif step in ("GXS", "GXD") and not last:
                    gather_group("src" if step == "GXS" else "dst", i + 1, first=False)
                if "." not in step:
                    return
                slot, what = step.split(".")
                n = SLOTS.index(slot)
                j = JOBS * i + n
                edge = slot[0] == "E"
                R = ET if edge else P
                if what == "xb":
                    if not edge:
                        gate(f"xin_loaded{n % 2}", 16 * (2 * i + n // 2 + 1))
                    else:
                        gate("xe_done", 2 * i + n - 3)
                    source = xe[:, 2 * n - 8:2 * n - 6, :] if edge else xin[n % 2]
                    gate("y_done", j)
                    pool.tensor_tensor(xb[n % 2][0:R, :, :], source[0:R, :, :],
                                       be2_all[0:R, :].rearrange("p (a d) -> p a d", a=1).broadcast_to([R, 2, D]), ALU.add)\
                        .then_inc(s["xb_done"], 1)
                elif what == "xr":
                    gate("n1_done", j + 2)
                    gate("t_done", j)
                    gate("sq2_done", j)
                    pool.tensor_tensor(x2[n % 2][0:R, :, :], n1[n % 2][0:R, :, :],
                                       g1_all[0:R, :].rearrange("p (a d) -> p a d", a=1).broadcast_to([R, 2, D]), ALU.mult)\
                        .then_inc(s["xr_done"], 1)
                elif what == "out":
                    gate("z_rows", j + 2)
                    gate("last_picked" if edge else "node_picked", i + 1)
                    for t in range(2):
                        if edge:
                            scatter(y[n % 2][0:R, t, :], last_now[:, 2 * (n - 4) + t:2 * (n - 4) + t + 1], f"out_{slot}")
                        else:
                            scatter(y[n % 2][0:R, t, :], node_now[:, 2 * n + t:2 * n + t + 1], f"out_{slot}")

            for n, (w, name) in enumerate(((wv, "v"), (wo, "o"))):
                for k in range(KC):
                    pool.wait_ge(s["split_hi"], (2 + n) * KC + k + 1)
                    dest, hi, whole = w[1][:, k, :], w[0][:, k, :].bitcast(F32), w_stage[name][:, k, :]
                    if name == "v":
                        dest, hi = (t.rearrange("p (m h d) -> p m h d", m=KC, h=HEADS) for t in (dest, hi))
                        whole = whole.rearrange("p (h m d) -> p m h d", h=HEADS, m=KC)
                    for m in range(KC) if name == "v" else [slice(None)]:
                        ins = pool.tensor_tensor(dest[:, m], whole[:, m], hi[:, m], ALU.subtract)
                    ins.then_inc(s["split_lo_pool"], 1)
            pool.wait_ge(s["all_loaded"], 48)
            pool.sem_inc(s["xr_done"], 1)
            run(pool, gate, ORDER["pool"], one_step, last_differs=True)
            for slot in SLOTS:
                pool.wait_ge(s[f"out_{slot}"], 32 * ROUNDS)

        @block.scalar
        def _(act):
            def wait(name, value):
                act.wait_ge(s[name], value)
                act.sem_inc(s["gate_act"], 1)

            gate = Waits(wait)

            def by_head(ap, k):
                return ap[:, k, :].rearrange("p (h m d) -> p m h d", h=HEADS, m=KC)

            def split_hi(w, stage, loaded, permute):
                act.wait_ge(s[loaded], 16 if loaded != "wo_loaded" else 16 * HEADS)
                for k in range(KC):
                    dest = w[0][:, k, :]
                    if permute:
                        act.activation(dest.rearrange("p (m h d) -> p m h d", m=KC, h=HEADS), by_head(stage, k), ACT.Copy)\
                            .then_inc(s["split_hi"], 1)
                    else:
                        act.activation(dest, stage[:, k, :], ACT.Copy).then_inc(s["split_hi"], 1)

            act.preload_act_table(ACT.Sqrt)
            split_hi(wq, w_stage["q"], "wq_loaded", True)
            split_hi(wk, w_stage["k"], "wk_loaded", True)
            split_hi(wv, w_stage["v"], "wv_loaded", True)
            split_hi(wo, w_stage["o"], "wo_loaded", False)
            act.wait_ge(s["init_done"], 4)

            def one_step(i, step):
                if step[:2] == "TX":
                    gate("tr_filled", FILLS * i + FILL[step] + 1)
                    if step[:3] == "TXD":
                        gate("pj_filled", 16 * i - 4)
                    else:
                        gate("pj_filled", 16 * i + 4)
                    act.activation(xT[0][:, int(step[3]), :], pT[FILL[step] % 2][:, 0:EG], ACT.Copy).then_inc(s["xT_hi"], 1)
                elif step[:2] == "CP":
                    half = int(step[2])
                    gate("xd_loaded", 64 * (i + 1))
                    gate("hx_done", 4 * i)
                    gate("xb_done", JOBS * i)
                    act.activation(xe[:, 2 * half:2 * half + 2, :], xd[:, 2 * half:2 * half + 2, :], ACT.Copy).then_inc(s["xe_done"], 1)
                elif step[0] == "Q":
                    m = int(step[1])
                    gate("pj_filled", 16 * i + m + 1)
                    gate("rzb_done", i)
                    gate("carried", 4 * i)
                    act.activation(q[:, m, 0:EG], bank(step)[:, 0:EG], ACT.Copy).then_inc(s["q_saved"], 1)
                elif step == "S":
                    act.preload_act_table(ACT.Exp)
                    gate("decay_done", i + 1)
                    gate("weight_exp", i + 1)
                    act.activation(ex[:, :, :], ex[:, :, :], ACT.Exp).then_inc(s["exp_done"], 1)
                    act.preload_act_table(ACT.Sqrt)
                elif step[0] == "V":
                    m = int(step[1])
                    gate("scanned", 4 * i + m + 1)
                    gate("pj_filled", 16 * i)
                    act.activation(aT[0][:, m, :], att[:, m % 2, :], ACT.Copy).then_inc(s["a_hi"], 1)
                if "." not in step:
                    return
                slot, what = step.split(".")
                n = SLOTS.index(slot)
                j = JOBS * i + n
                edge = slot[0] == "E"
                R = ET if edge else P

                def deviation(c, var, scale):
                    gate(f"rs{c}_done", j)
                    act.activation(sd[c - 1][n % 2][0:R, :], var, ACT.Sqrt, bias=eps_col[0:R, :], scale=scale)\
                        .then_inc(s[f"sd{c}_done"], 1)

                def squares_of(c, source):
                    gate(f"nm{c}_done", j + 1)
                    gate(f"sd{c}_done", j + 1)
                    for t in range(2):
                        ins = act.activation(squares[c - 1][0:R, t, :], source[0:R, t, :], ACT.Square,
                                             bias=nmean[c - 1][n % 2][0:R, t:t + 1], accum_out=sq[c - 1][0:R, t:t + 1])
                    ins.then_inc(s[f"sq{c}_done"], 1)
                    gate(f"sq{c}_done", j + 1 + (c == 2))
                    deviation(c, sq[c - 1][0:R, :], 1.0 / D)

                if what == "sd":
                    gate("mv1_done", 2 * j + 2)
                    deviation(1, mv[n % 2][0:R, :, 1], 1.0)
                elif what == "T":
                    for half in range(2):
                        fill = FILL[step] + half
                        gate("tr_filled", FILLS * i + fill + 1)
                        gate("h_filled", j + 1)
                        act.activation(nT[:, 2 * half:2 * half + 2, 0:2 * R],
                                       pT[fill % 2][:, :].rearrange("p (a n) -> p a n", a=2)[:, :, 0:2 * R], ACT.Copy)\
                            .then_inc(s["nT_done"], 1)
                elif what == "F1":
                    gate("h_filled", j + 2)
                    gate("f_filled", 2 * j)
                    act.activation(hT[0:DFF, 0:2 * R], pF[0][0:DFF, 0:2 * R], ACT.Relu, bias=b1_col[:, :]).then_inc(s["h_done"], 1)
                elif what == "sq":
                    gate("sq2_done", j + 1)
                    squares_of(2, x2[n % 2])
                elif what == "sq3":
                    gate("sq3_done", j)
                    squares_of(3, y[n % 2])
                elif what == "z":
                    gate("shift3_done", j + 1)
                    gate("sq3_done", j + 1)
                    for t in range(2):
                        ins = act.activation(y[n % 2][0:R, t, :], y[n % 2][0:R, t, :], ACT.Identity,
                                             scale=rs[2][n % 2][0:R, t:t + 1], bias=shift[2][n % 2][0:R, t:t + 1])
                    ins.then_inc(s["z_rows"], 1)

            act.sem_inc(s["sq2_done"], 1)
            act.sem_inc(s["z_rows"], 1)
            for c in (1, 2, 3):
                act.sem_inc(s[f"sd{c}_done"], 1)
            run(act, gate, ORDER["act"], one_step)

        @block.vector
        def _(dve):
            def wait(name, value):
                dve.wait_ge(s[name], value)
                dve.sem_inc(s["gate_dve"], 1)

            gate = Waits(wait)

            def by_head(ap, k):
                return ap[:, k, :].rearrange("p (h m d) -> p m h d", h=HEADS, m=KC)

            dve.wait_ge(s["idx_loaded"], 64)
            dve.tensor_copy(idx_f[0:CT, :, :], idx_raw[0:CT, :, :]).then_inc(s["idx_cast"], 1)
            turned = pF[1][0:ET, 0:3 * CT].rearrange("p (a t) -> p a t", a=3)
            dve.wait_ge(s["idx_turned"], 1)
            dve.tensor_copy(src_idx[:, :], turned[:, 0, :]).then_inc(s["idx_done"], 1)
            dve.tensor_copy(dst_idx[:, :], turned[:, 1, :]).then_inc(s["idx_done"], 1)
            dve.tensor_copy(col_f[0:ET, :], turned[:, 2, :]).then_inc(s["last_flag"], 1)
            dve.wait_ge(s["last_flag"], 1)
            dve.tensor_tensor(part_f[0:ET, :], turned[:, 1, :], col_f[0:ET, :], ALU.is_equal).then_inc(s["last_flag"], 1)
            dve.wait_ge(s["last_flag"], 2)
            dve.scalar_tensor_tensor(last_idx[:, :], part_f[0:ET, :], float(SKIP), turned[:, 1, :], ALU.mult, ALU.add)\
                .then_inc(s["idx_done"], 1)

            def split_lo(w, stage, splits):
                for k in range(KC):
                    dve.wait_ge(s["split_hi"], splits + k + 1)
                    view = lambda t: t[:, k, :].rearrange("p (m h d) -> p m h d", m=KC, h=HEADS)
                    for m in range(KC):
                        ins = dve.tensor_tensor(view(w[1])[:, m], by_head(stage, k)[:, m], view(w[0])[:, m].bitcast(F32), ALU.subtract)
                    ins.then_inc(s["split_lo"], 1)

            dve.wait_ge(s["w1_loaded"], 64)
            for k in range(KC):
                dve.tensor_scalar(w1[:, k, :], w1_raw[:, k, :], g1_col[:, k:k + 1], None, ALU.mult).then_inc(s["w1_done"], 1)
            split_lo(wq, w_stage["q"], 0)
            dve.memset(hT[DFF:DFF + 1, :], 1.0).then_inc(s["ones_set"], 1)
            dve.wait_ge(s["w2_loaded"], 48)
            dve.tensor_tensor(w2[DFF:DFF + 1, :], w2[DFF:DFF + 1, :], be1_row, ALU.add).then_inc(s["w2_done"], 1)
            dve.wait_ge(s["b1_folded"], 1)
            dve.tensor_tensor(b1_col[:, :], pF[0][0:DFF, 0:1], b1_col[:, :], ALU.add).then_inc(s["b1_done"], 1)
            split_lo(wk, w_stage["k"], KC)
            dve.wait_ge(s["iota_set"], 2)
            dve.tensor_copy(iota_b, iota_i).then_inc(s["iota_cast"], 1)
            dve.wait_ge(s["idx_done"], 3)
            dve.tensor_scalar(part_i[0:ET, :], dst_idx[:, :], 1, P - 1, ALU.logical_shift_right, ALU.bitwise_and).then_inc(s["digit_low"], 1)
            dve.tensor_scalar(col_i[0:ET, :], dst_idx[:, :], 8, 1, ALU.logical_shift_right, ALU.logical_shift_left).then_inc(s["digit_low"], 1)
            dve.tensor_scalar(low_i[0:ET, :], dst_idx[:, :], 1, None, ALU.bitwise_and).then_inc(s["digit_low"], 1)
            dve.wait_ge(s["digit_low"], 3)
            dve.tensor_copy(part_b[0:ET, :], part_i[0:ET, :]).then_inc(s["digit_done"], 1)
            dve.tensor_tensor(col_b[0:ET, :], col_i[0:ET, :], low_i[0:ET, :], ALU.add).then_inc(s["digit_done"], 1)
            dve.wait_ge(s["digit_done"], 2)
            dve.wait_ge(s["iota_cast"], 1)
            for c in range(CT // OHT):
                if c >= 2:
                    dve.wait_ge(s["counted"], c - 1)
                for oh, digit, width in zip(onehots[c % 2], (part_b, col_b), (P, CN)):
                    dve.tensor_tensor(oh, iota_b[0:ET, 0:width].rearrange("p (a n) -> p a n", a=1).broadcast_to([ET, OHT, width]),
                                      digit[0:ET, OHT * c:OHT * c + OHT].rearrange("p (t a) -> p t a", a=1).broadcast_to([ET, OHT, width]),
                                      ALU.is_equal).then_inc(s["onehot"], 1)
            dve.wait_ge(s["counted"], CT // OHT)
            dve.tensor_scalar(has_edge, pS[:, 0:CN], 0.5, float(SKIP), ALU.is_gt, ALU.mult).then_inc(s["flag_done"], 1)
            dve.wait_ge(s["flag_done"], 1)
            dve.tensor_tensor(node_idx[:, :], has_edge, node_i, ALU.add).then_inc(s["node_done"], 1)

            for name in ("n1_done", "t_done", "y_done", "rs1_done", "rs2_done", "rs3_done"):
                dve.sem_inc(s[name], 1)

            def one_step(i, step):
                if step == "TXD":
                    gate("row_loaded", 16 * (i + 1))
                    gate("alpha_done", i)
                    dve.tensor_tensor(nsame[:, :], dst_row[:, 1:EG + 1], dst_row[:, 0:EG], ALU.is_equal).then_inc(s["mask_eq"], 1)
                elif step[:2] == "TX":
                    k, fill = int(step[3]), FILL[step]
                    if step[:3] == "TXD":
                        gate("xT_hi", 2 * KC * i + k + 1)
                        gate("pj_filled", 16 * i - 4)
                    else:
                        gate("xT_hi", 2 * KC * i + KC + k + 1)
                        gate("pj_filled", 16 * i + 4)
                    dve.tensor_tensor(xT[1][:, k, :], pT[fill % 2][:, 0:EG], xT[0][:, k, :].bitcast(F32), ALU.subtract)\
                        .then_inc(s["xT_lo"], 1)
                elif step[0] == "K":
                    m = int(step[1])
                    gate("pj_filled", 16 * i + 4 + m + 1)
                    gate("q_saved", 4 * i + m + 1)
                    if m == 0:
                        gate("score_done", i)
                    else:
                        gate("qk_acc", 3 * i + m - 1)
                    dve.tensor_tensor((qk if m == 0 else qk_m)[:, :], bank(step)[:, 0:EG], q[:, m, 0:EG], ALU.mult)\
                        .then_inc(s["qk_part"], 1)
                elif step == "S":
                    gate("score_done", i + 1)
                    gate("mask_done", 2 * i + 2)
                    gate("max_carried", i)
                    dve.tensor_tensor_scan(mx[:, 1:EG + 1], far[:, :], pS[:, 0:EG], mx[:, 0:1], ALU.add, ALU.max)\
                        .then_inc(s["max_done"], 1)
                elif step == "EX":
                    gate("max_done", i + 1)
                    gate("alpha_done", i)
                    gate("scanned", 4 * i)
                    dve.tensor_tensor(ex[:, 0, :], mx[:, 0:EG], far[:, :], ALU.add).then_inc(s["decay_half"], 1)
                    dve.tensor_tensor(ex[:, 1, :], pS[:, 0:EG], mx[:, 1:EG + 1], ALU.subtract).then_inc(s["weight_exp"], 1)
                    gate("decay_half", i + 1)
                    dve.tensor_tensor(ex[:, 0, :], ex[:, 0, :], mx[:, 1:EG + 1], ALU.subtract).then_inc(s["decay_done"], 1)
                elif step == "MC":
                    gate("decay_done", i + 1)
                    gate("weight_exp", i + 1)
                    dve.tensor_copy(mx[:, 0:1], mx[:, EG:EG + 1]).then_inc(s["max_carried"], 1)
                elif step == "Z":
                    gate("exp_done", i + 1)
                    gate("z_carried", i)
                    gate("zT_done", i)
                    dve.tensor_tensor_scan(zs[:, 1:EG + 1], ex[:, 0, :], ex[:, 1, :], zs[:, 0:1], ALU.mult, ALU.add)\
                        .then_inc(s["z_done"], 1)
                elif step == "ZC":
                    gate("z_done", i + 1)
                    dve.tensor_copy(zs[:, 0:1], zs[:, EG:EG + 1]).then_inc(s["z_carried"], 1)
                elif step == "ZT":
                    gate("zT_done", i + 1)
                    dve.reciprocal(rz[:, :, :], pS[0:ET, :].rearrange("p (t h d) -> p t h d", t=4, h=HEADS)[:, :, :, 0])\
                        .then_inc(s["rz_done"], 1)
                    gate("rz_done", i + 1)
                    gate("rzb_done", i)
                    dve.tensor_copy(rz_all[:, :, :].rearrange("p t (h d) -> p (t h) d", h=HEADS),
                                    rz[:, :, :].rearrange("p t (h a) -> p (t h) a", a=1).broadcast_to([ET, 4 * HEADS, HD]))\
                        .then_inc(s["rz_spread"], 1)
                elif step == "RZ":
                    gate("rzb_done", i + 1)
                    dve.tensor_tensor(ex[:, 1, :], pS[:, 0:EG], ex[:, 1, :], ALU.mult).then_inc(s["beta_done"], 1)
                    gate("beta_done", i + 1)
                    dve.scalar_tensor_tensor(ex[:, 0, :], ex[:, 1, :], 1.0, nsame[:, :], ALU.subtract, ALU.mult)\
                        .then_inc(s["alpha_done"], 1)
                elif step[0] == "H":
                    o = int(step[1])
                    n = o // 2
                    gate("tr_filled", FILLS * i + END["C.T" if n == 0 else "D.T"])
                    gate("xr_done", JOBS * i + 4 + n)
                    gate("xe_done", 2 * i + n + 1)
                    gate("pj_filled", 16 * i + 12 + o + 1)
                    dve.tensor_tensor(n1[n][0:ET, o % 2, :], bank(f"O{o}")[0:ET, :], xe[:, o, :], ALU.add)\
                        .then_inc(s["hx_done"], 1)
                elif step[0] == "W":
                    m = int(step[1])
                    gate("pj_filled", 16 * i + 8 + m + 1)
                    gate("beta_done", i + 1)
                    gate("scanned", 4 * i + max(m - 1, 0))
                    dve.tensor_tensor(wgt[:, m % 2, :], bank(f"V{m}")[:, 0:EG], ex[:, 1, :], ALU.mult).then_inc(s["weighted"], 1)
                elif step[0] == "N":
                    m = int(step[1])
                    gate("weighted", 4 * i + m + 1)
                    gate("alpha_done", i + 1)
                    gate("a_lo", 4 * i + max(m - 1, 0))
                    gate("carried", 4 * i + max(m - 1, 0))
                    dve.tensor_tensor_scan(att[:, m % 2, :], ex[:, 0, :], wgt[:, m % 2, :], carry[:, m:m + 1], ALU.mult, ALU.add)\
                        .then_inc(s["scanned"], 1)
                elif step[0] == "G":
                    m = int(step[1])
                    gate("scanned", 4 * i + m + 1)
                    dve.tensor_copy(carry[:, m:m + 1], att[:, m % 2, EG - 1:EG]).then_inc(s["carried"], 1)
                elif step[0] == "L":
                    m = int(step[1])
                    gate("a_hi", 4 * i + m + 1)
                    gate("pj_filled", 16 * i)
                    dve.tensor_tensor(aT[1][:, m, :], att[:, m % 2, :], aT[0][:, m, :].bitcast(F32), ALU.subtract)\
                        .then_inc(s["a_lo"], 1)
                if "." not in step:
                    return
                slot, what = step.split(".")
                n = SLOTS.index(slot)
                j = JOBS * i + n
                edge = slot[0] == "E"
                R = ET if edge else P

                def inverse(c):
                    gate(f"sd{c}_done", j + 2)
                    gate({1: "n1_done", 2: "y_done", 3: "z_rows"}[c], j)
                    dve.reciprocal(rs[c - 1][n % 2][0:R, :], sd[c - 1][n % 2][0:R, :]).then_inc(s[f"rs{c}_done"], 1)

                if what == "sum1":
                    if edge:
                        gate("hx_done", 4 * i + 2 * (n - 4) + 2)
                    else:
                        gate(f"xin_loaded{n % 2}", 16 * (2 * i + n // 2 + 1))
                    source = n1[n % 2] if edge else xin[n % 2]
                    gate("mv1_done", 2 * j)
                    for t in range(2):
                        dve.bn_stats(st[0:R, t, :], source[0:R, t, :]).then_inc(s["st1_done"], 1)
                elif what == "mv":
                    gate("sd1_done", j)
                    gate("n1_done", j)
                    for t in range(2):
                        gate("st1_done", 2 * j + t + 1)
                        dve.bn_aggr(mv[n % 2][0:R, t, :], st[0:R, t, :]).then_inc(s["mv1_done"], 1)
                elif what in ("r1", "r2", "r3"):
                    inverse(int(what[1]))
                elif what == "norm1":
                    gate("rs1_done", j + 2)
                    if not edge:
                        if n == 1:
                            gate("split_lo_pool", 0 * i + KC)
                        gate("h_filled", j)
                        gate("xr_done", j)
                    source = n1[n % 2] if edge else xin[n % 2]
                    for t in range(2):
                        ins = dve.tensor_scalar(n1[n % 2][0:R, t, :], source[0:R, t, :], mv[n % 2][0:R, t, 0:1], rs[0][n % 2][0:R, t:t + 1],
                                                ALU.subtract, ALU.mult)
                    ins.then_inc(s["n1_done"], 1)
                elif what == "x2":
                    gate("xr_done", j + 2)
                    gate("nm2_done", j)
                    for t in range(2):
                        gate("f_filled", 2 * j + t + 1)
                        dve.scalar_tensor_tensor(x2[n % 2][0:R, t, :], pF[(t + 1) % 2][0:R, :], 1.0, x2[n % 2][0:R, t, :],
                                                 ALU.mult, ALU.add, accum_out=sums[1][0:R, t:t + 1]).then_inc(s["x2_done"], 1)
                elif what == "m2":
                    gate("x2_done", 2 * j + 2)
                    gate("t_done", j)
                    gate("sq2_done", j)
                    dve.tensor_scalar(nmean[1][n % 2][0:R, :], sums[1][0:R, :], -1.0 / D, None, ALU.mult).then_inc(s["nm2_done"], 1)
                elif what == "t":
                    if n == 0:
                        gate("split_lo_pool", 0 * i + 2 * KC)
                    gate("nm2_done", j + 1)
                    gate(f"out_{SLOTS[n - 2]}", 32 * (i + (n >= 2)))
                    for t in range(2):
                        ins = dve.scalar_tensor_tensor(y[n % 2][0:R, t, :], x2[n % 2][0:R, t, :], nmean[1][n % 2][0:R, t:t + 1], g2_all[0:R, :],
                                                       ALU.add, ALU.mult)
                    ins.then_inc(s["t_done"], 1)
                elif what == "y":
                    gate("t_done", j + 2)
                    gate("rs2_done", j + 2)
                    gate("xb_done", j + 1)
                    gate("nm3_done", j)
                    for t in range(2):
                        ins = dve.scalar_tensor_tensor(y[n % 2][0:R, t, :], y[n % 2][0:R, t, :], rs[1][n % 2][0:R, t:t + 1], xb[n % 2][0:R, t, :],
                                                       ALU.mult, ALU.add, accum_out=sums[2][0:R, t:t + 1])
                    ins.then_inc(s["y_done"], 1)
                elif what == "m3":
                    gate("y_done", j + 2)
                    gate("z_rows", j)
                    dve.tensor_scalar(nmean[2][n % 2][0:R, :], sums[2][0:R, :], -1.0 / D, None, ALU.mult).then_inc(s["nm3_done"], 1)
                elif what == "shift":
                    gate("rs3_done", j + 2)
                    gate("nm3_done", j + 1)
                    dve.tensor_tensor(shift[2][n % 2][0:R, :], nmean[2][n % 2][0:R, :], rs[2][n % 2][0:R, :], ALU.mult)\
                        .then_inc(s["shift3_done"], 1)

            run(dve, gate, ORDER["dve"], one_step)

        @block.tensor
        def _(pe):
            pe.wait_ge(s["ident_done"], 1)
            pe.wait_ge(s["idx_cast"], 1)
            turned = pF[1][0:ET, 0:3 * CT].rearrange("p (a t) -> p a t", a=3)
            for a in range(3):
                ins = pe.transpose(turned[:, a, :], idx_f[0:CT, a, :], ident[0:CT, 0:CT])
            ins.then_inc(s["idx_turned"], 1)
            pe.wait_ge(s["w1_loaded"], 64)
            for k in range(KC):
                ins = pe.matmul(pF[0][0:DFF, 0:1], w1_raw[:, k, :], be1_col[:, k:k + 1], start=(k == 0), stop=(k == KC - 1))
            ins.then_inc(s["b1_folded"], 1)
            for c in range(CT // OHT):
                pe.wait_ge(s["onehot"], 2 * c + 2)
                for t in range(OHT):
                    ins = pe.matmul(pS[:, 0:CN], onehots[c % 2][0][:, t, :], onehots[c % 2][1][:, t, :], start=(c + t == 0), stop=(c == CT // OHT - 1 and t == OHT - 1))
                ins.then_inc(s["counted"], 1)
            pe.wait_ge(s["head_done"], 1)
            pe.wait_ge(s["ones_set"], 1)
            pe.wait_ge(s["b1_done"], 1)
            pe.wait_ge(s["w1_done"], KC)
            pe.wait_ge(s["w2_done"], 1)

            gate = Waits(lambda name, value: pe.wait_ge(s[name], value))

            def split_product(acc, left, right, n):
                for k in range(n):
                    for a, b in ((0, 0), (0, 1), (1, 0)):
                        ins = pe.matmul(acc, left(a, k), right(b, k), start=(k == 0 and a == b), stop=(k == n - 1 and a == 1))
                return ins

            def one_step(i, step):
                def bank_free(fill):
                    kind, count = READER[fill]
                    gate(kind, (2 * KC if kind == "xT_lo" else 2 * JOBS) * i + count)

                if step in ("Q0", "K0"):
                    gate("split_lo", 0 * i + (KC if step == "Q0" else 2 * KC))
                if step in ("V0", "O0"):
                    gate("split_lo_pool", 0 * i + (KC if step == "V0" else 2 * KC))
                if step == "S":
                    gate("flag_done", 0 * i + 1)
                if step[:2] == "TX":
                    rows_in = xd if step[:3] == "TXD" else xs
                    k, fill = int(step[3]), FILL[step]
                    if k == 0:
                        gate("xd_loaded" if step[:3] == "TXD" else "xs_loaded", 64 * (i + 1))
                    bank_free(fill)
                    for t in range(4):
                        ins = pe.transpose(pT[fill % 2][:, ET * t:ET * t + ET], rows_in[:, t, P * k:P * k + P], ident[0:ET, 0:ET])
                    ins.then_inc(s["tr_filled"], 1)
                elif "." not in step and step[0] in "QKV":
                    m = int(step[1])
                    w = {"Q": wq, "K": wk, "V": wv}[step[0]]
                    gate("xT_lo", 2 * KC * i + (KC if step[0] == "Q" else 2 * KC))
                    free_bank(i, PLACE[step])
                    split_product(bank(step)[:, 0:EG], lambda a, k: w[a][:, k, P * m:P * m + P], lambda b, k: xT[b][:, k, :], KC)\
                        .then_inc(s["pj_filled"], 1)
                elif step == "S":
                    gate("qk_acc", 3 * i + 3)
                    gate("beta_done", i)
                    pe.matmul(pS[:, 0:EG], same_head[:, :], qk[:, :], start=True, stop=True).then_inc(s["score_done"], 1)
                elif step == "ZT":
                    gate("z_done", i + 1)
                    gate("weight_exp", i + 1)
                    for t in range(4):
                        ins = pe.transpose(pS[0:ET, P * t:P * t + P], zs[:, 1 + ET * t:1 + ET * t + ET], ident[:, :])
                    ins.then_inc(s["zT_done"], 1)
                elif step == "RZ":
                    gate("rz_spread", i + 1)
                    for t in range(4):
                        ins = pe.transpose(pS[:, ET * t:ET * t + ET], rz_all[:, t, :], ident[0:ET, 0:ET])
                    ins.then_inc(s["rzb_done"], 1)
                elif "." not in step and step[0] == "O":
                    t = int(step[1])
                    gate("a_lo", 4 * i + 4)
                    free_bank(i, PLACE[step])
                    split_product(bank(step)[0:ET, :], lambda a, m: aT[a][:, m, ET * t:ET * t + ET], lambda b, m: wo[b][:, m, :], KC)\
                        .then_inc(s["pj_filled"], 1)
                if "." not in step:
                    return
                slot, what = step.split(".")
                n = SLOTS.index(slot)
                j = JOBS * i + n
                edge = slot[0] == "E"
                R = ET if edge else P
                if what == "T":
                    gate("n1_done", j + 2)
                    for half in range(2):
                        fill = FILL[step] + half
                        bank_free(fill)
                        for c in range(2):
                            k = 2 * half + c
                            for t in range(2):
                                ins = pe.transpose(pT[fill % 2][:, NB * c + R * t:NB * c + R * t + R], n1[n % 2][0:R, t, P * k:P * k + P], ident[0:R, 0:R])
                        ins.then_inc(s["tr_filled"], 1)
                elif what == "F1":
                    gate("nT_done", 2 * j + 2)
                    gate("x2_done", 2 * j)
                    for k in range(KC):
                        ins = pe.matmul(pF[0][0:DFF, 0:2 * R], w1[:, k, :], nT[:, k, 0:2 * R], start=(k == 0), stop=(k == KC - 1))
                    ins.then_inc(s["h_filled"], 1)
                elif what == "F2":
                    gate("h_done", j + 1)
                    for t in range(2):
                        pe.matmul(pF[(t + 1) % 2][0:R, :], hT[:, R * t:R * t + R], w2[:, :], start=True, stop=True)\
                            .then_inc(s["f_filled"], 1)

            kinds, counts = [], {"xT_lo": 0, "nT_done": 0}
            for step in pe_steps:
                for _ in range(END[step] - FILL[step] if step in FILL else 0):
                    kinds.append("xT_lo" if step[0] == "T" else "nT_done")
            assert kinds[-2:] == ["nT_done"] * 2
            READER = [("nT_done", -1), ("nT_done", 0)]
            for kind in kinds[:-2]:
                counts[kind] += 1
                READER.append((kind, counts[kind]))

            def free_bank(i, place):
                before = [n for n in range(place) if BANK[n] == BANK[place]]
                if before:
                    kind, m = divmod(before[-1], 4)
                    gate(("q_saved", "qk_part", "weighted", "hx_done")[kind], 4 * i + m + 1)
                else:
                    last = max(n for n in range(12, 16) if BANK[n] == BANK[place])
                    gate("hx_done", 4 * i - (15 - last))

            pe.sem_inc(s["h_filled"], 1)
            run(pe, gate, ORDER["pe"], one_step)


_INS = ["x", "src", "dst", "L0_gnn_Wq", "L0_gnn_Wk", "L0_gnn_Wv", "L0_gnn_Wo", "L0_gnn_ln1_g", "L0_gnn_ln1_b",
        "L0_gnn_ln2_g", "L0_gnn_ln2_b", "L0_gnn_W1", "L0_gnn_b1", "L0_gnn_W2", "L0_gnn_b2"]


def kernel(**inputs):
    import numpy as _np
    import concourse.bacc as _bacc
    from concourse import mybir as _mybir
    from concourse.bass_utils import run_bass_kernel_spmd as _run

    nc = _bacc.Bacc("TRN2", target_bir_lowering=False, num_devices=1)
    arrays, args = {}, []
    for name in _INS:
        a = _np.ascontiguousarray(inputs[name])
        arrays[f"in_{name}_dram"] = a
        args.append(nc.dram_tensor(f"in_{name}_dram", a.shape, _mybir.dt.from_np(a.dtype), kind="ExternalInput").ap())
    out = nc.dram_tensor("out_0_dram", inputs["x"].shape, _mybir.dt.float32, kind="ExternalOutput").ap()
    graph_attention(nc, *args, out)
    r = _run(nc, [arrays], core_ids=[0])
    return r.results[0]["out_0_dram"]
```
